# Optimizing a Trainium2 kernel written in Bass

```python
import numpy as np
import jax
import jax.numpy as jnp

def _softmax(x, axis=-1):
    return jax.nn.softmax(x, axis=axis)

def _gelu(x):
    return jax.nn.gelu(x, approximate=True)

def _silu(x):
    return jax.nn.silu(x)

def _sigmoid(x):
    return jax.nn.sigmoid(x)

def _layernorm(x, axis=-1, eps=1e-05):
    m = jnp.mean(x, axis=axis, keepdims=True)
    v = jnp.var(x, axis=axis, keepdims=True)
    return (x - m) / jnp.sqrt(v + eps)

def _scatter_add(tgt, idx, src, axis=0):
    return tgt.at[idx].add(src)

def _segment_sum(src, seg, n):
    return jax.ops.segment_sum(src, seg, n)
kernel_name = 'mk_seq_postln_d1_jaxref_r8_ab09dc'

def setup_inputs(seed: int=0):
    np.random.seed(seed)
    _w = jnp.asarray

    def _L0_attn_setup():
        import jax, jax.numpy as jnp
        import numpy as np
        EPS = 1e-06
        H = 16

        def rmsnorm(x, w):
            return x * jax.lax.rsqrt(jnp.mean(x * x, axis=-1, keepdims=True) + EPS) * w

        def l2norm(x):
            return x * jax.lax.rsqrt(jnp.sum(x * x, axis=-1, keepdims=True) + EPS)

        def delta_rule(q, k, v, beta):
            B, S, Hh, dk = q.shape
            dv = v.shape[-1]
            qt = jnp.moveaxis(q, 1, 0)
            kt = jnp.moveaxis(k, 1, 0)
            vt = jnp.moveaxis(v, 1, 0)
            bt = jnp.moveaxis(beta, 1, 0)

            def step(Sm, inp):
                qi, ki, vi, bi = inp
                Sk = jnp.einsum('bhkv,bhk->bhv', Sm, ki)
                upd = ki[..., :, None] * (vi - Sk)[..., None, :]
                Sm = Sm + bi[..., None, None] * upd
                oi = jnp.einsum('bhkv,bhk->bhv', Sm, qi)
                return (Sm, oi)
            S0 = jnp.zeros((B, Hh, dk, dv), q.dtype)
            _, out = jax.lax.scan(step, S0, (qt, kt, vt, bt))
            return jnp.moveaxis(out, 0, 1)
        key = jax.random.key(seed)
        ks = jax.random.split(key, 12)
        B, S, D, F = (2, 256, 128, 512)
        std = 0.02
        inp = {'hidden_states': jax.random.normal(ks[0], (B, S, D), jnp.float32), 'Wq': jax.random.normal(ks[1], (D, D), jnp.float32) * std, 'Wk': jax.random.normal(ks[2], (D, D), jnp.float32) * std, 'Wv': jax.random.normal(ks[3], (D, D), jnp.float32) * std, 'Wb': jax.random.normal(ks[4], (D, H), jnp.float32) * std, 'Wo': jax.random.normal(ks[5], (D, D), jnp.float32) * std, 'ln1': jnp.ones((D,), jnp.float32), 'ln2': jnp.ones((D,), jnp.float32), 'Wg': jax.random.normal(ks[6], (D, F), jnp.float32) * std, 'Wu': jax.random.normal(ks[7], (D, F), jnp.float32) * std, 'Wd': jax.random.normal(ks[8], (F, D), jnp.float32) * std}
        return inp
    _L0_attn_in = _L0_attn_setup()

    def _L0_ffn_setup():
        import jax, jax.numpy as jnp
        import numpy as np
        FP8_MAX = 448.0
        key = jax.random.key(seed)
        k_x, k_w, k_b = jax.random.split(key, 3)
        B, S, IN, OUT = (4, 1024, 128, 128)
        x = jax.random.normal(k_x, (B, S, IN), dtype=jnp.float32)
        w_fp32 = jax.random.normal(k_w, (OUT, IN), dtype=jnp.float32)
        weight_fp8 = w_fp32.astype(jnp.float8_e4m3fn).astype(jnp.float32)
        bias = jax.random.normal(k_b, (OUT,), dtype=jnp.float32)
        input_scale = jnp.ones((1,), dtype=jnp.float32)
        weight_scale = jnp.ones((1,), dtype=jnp.float32)
        return {'x': x, 'weight_fp8': weight_fp8, 'bias': bias, 'input_scale': input_scale, 'weight_scale': weight_scale}
    _L0_ffn_in = _L0_ffn_setup()
    _d = {'L0_attn_hidden_states': _L0_attn_in['hidden_states'], 'L0_attn_Wq': _L0_attn_in['Wq'], 'L0_attn_Wk': _L0_attn_in['Wk'], 'L0_attn_Wv': _L0_attn_in['Wv'], 'L0_attn_Wb': _L0_attn_in['Wb'], 'L0_attn_Wo': _L0_attn_in['Wo'], 'L0_attn_ln1': _L0_attn_in['ln1'], 'L0_attn_ln2': _L0_attn_in['ln2'], 'L0_attn_Wg': _L0_attn_in['Wg'], 'L0_attn_Wu': _L0_attn_in['Wu'], 'L0_attn_Wd': _L0_attn_in['Wd'], 'L0_ffn_weight_fp8': _L0_ffn_in['weight_fp8'], 'L0_ffn_bias': _L0_ffn_in['bias'], 'L0_ffn_input_scale': _L0_ffn_in['input_scale'], 'L0_ffn_weight_scale': _L0_ffn_in['weight_scale']}
    _x0 = _d['L0_attn_hidden_states']
    _d['L0_attn_hidden_states'] = jax.random.normal(jax.random.fold_in(jax.random.key(seed), 1), (16, 512, 128), dtype=_x0.dtype)
    del _x0
    return _d

def reference(L0_attn_hidden_states, L0_attn_Wq, L0_attn_Wk, L0_attn_Wv, L0_attn_Wb, L0_attn_Wo, L0_attn_ln1, L0_attn_ln2, L0_attn_Wg, L0_attn_Wu, L0_attn_Wd, L0_ffn_weight_fp8, L0_ffn_bias, L0_ffn_input_scale, L0_ffn_weight_scale):

    def _L0_attn_ref(hidden_states, Wq, Wk, Wv, Wb, Wo, ln1, ln2, Wg, Wu, Wd):
        import jax, jax.numpy as jnp
        import numpy as np
        EPS = 1e-06
        H = 16

        def rmsnorm(x, w):
            return x * jax.lax.rsqrt(jnp.mean(x * x, axis=-1, keepdims=True) + EPS) * w

        def l2norm(x):
            return x * jax.lax.rsqrt(jnp.sum(x * x, axis=-1, keepdims=True) + EPS)

        def delta_rule(q, k, v, beta):
            B, S, Hh, dk = q.shape
            dv = v.shape[-1]
            qt = jnp.moveaxis(q, 1, 0)
            kt = jnp.moveaxis(k, 1, 0)
            vt = jnp.moveaxis(v, 1, 0)
            bt = jnp.moveaxis(beta, 1, 0)

            def step(Sm, inp):
                qi, ki, vi, bi = inp
                Sk = jnp.einsum('bhkv,bhk->bhv', Sm, ki)
                upd = ki[..., :, None] * (vi - Sk)[..., None, :]
                Sm = Sm + bi[..., None, None] * upd
                oi = jnp.einsum('bhkv,bhk->bhv', Sm, qi)
                return (Sm, oi)
            S0 = jnp.zeros((B, Hh, dk, dv), q.dtype)
            _, out = jax.lax.scan(step, S0, (qt, kt, vt, bt))
            return jnp.moveaxis(out, 0, 1)
        B, S, D = hidden_states.shape
        dk = D // H
        x = rmsnorm(hidden_states, ln1)
        q = l2norm(jax.nn.silu(x @ Wq).reshape(B, S, H, dk))
        k = l2norm(jax.nn.silu(x @ Wk).reshape(B, S, H, dk))
        v = jax.nn.silu(x @ Wv).reshape(B, S, H, dk)
        beta = jax.nn.sigmoid(x @ Wb)
        o = delta_rule(q, k, v, beta).reshape(B, S, D)
        h = hidden_states + o @ Wo
        y = rmsnorm(h, ln2)
        h = h + jax.nn.silu(y @ Wg) * (y @ Wu) @ Wd
        return h

    def _L0_ffn_ref(x, weight_fp8, bias, input_scale, weight_scale):
        import jax, jax.numpy as jnp
        import numpy as np
        FP8_MAX = 448.0
        x_q = jnp.clip(x / input_scale, -FP8_MAX, FP8_MAX)
        x_dq = x_q.astype(jnp.float8_e4m3fn).astype(x.dtype) * input_scale
        w_dq = weight_fp8 * weight_scale
        out = jnp.einsum('bsi,oi->bso', x_dq, w_dq) + bias
        return out
    x = L0_attn_hidden_states
    x = _layernorm(x + _L0_attn_ref(x, L0_attn_Wq, L0_attn_Wk, L0_attn_Wv, L0_attn_Wb, L0_attn_Wo, L0_attn_ln1, L0_attn_ln2, L0_attn_Wg, L0_attn_Wu, L0_attn_Wd), axis=-1)
    x = _layernorm(x + _L0_ffn_ref(x, L0_ffn_weight_fp8, L0_ffn_bias, L0_ffn_input_scale, L0_ffn_weight_scale), axis=-1)
    return x

_drawn_inputs = setup_inputs


def setup_inputs(seed=0):
    import zlib

    import numpy as np

    out = dict(_drawn_inputs(seed))
    spreads = {'L0_attn_ln1': (1.0, 0.6), 'L0_attn_ln2': (1.0, 0.6)}
    factors = {'L0_attn_Wq': 3.12,
     'L0_attn_Wk': 3.108,
     'L0_attn_Wv': 3.086,
     'L0_attn_Wb': 8.0,
     'L0_attn_Wo': 3.096,
     'L0_attn_Wg': 3.544,
     'L0_attn_Wu': 3.528,
     'L0_attn_Wd': 3.534}
    for name, (base, spread) in spreads.items():
        noise = np.random.default_rng([zlib.crc32(name.encode()), seed]).standard_normal(out[name].shape)
        drawn = base * np.exp(spread * noise) if base else spread * noise
        out[name] = jnp.asarray(drawn.astype(out[name].dtype))
    for name, factor in factors.items():
        out[name] = (out[name] * factor).astype(out[name].dtype)
    return out
```

```python
from contextlib import ExitStack

import concourse.bass as bass
from concourse import mybir

P = 128
F32 = mybir.dt.float32
BF16 = mybir.dt.bfloat16
I32 = mybir.dt.int32
ALU = mybir.AluOpType
ACT = mybir.ActivationFunctionType
AX_X = mybir.AxisListType.X

RMS_EPS = 1e-6
LN_EPS = 1e-5
FP8_MAX = 448.0
FP8_MIN_NORMAL = 2.0 ** -6
EXPONENT_BITS = 0x7F800000
ROUND_TO_4_BITS = 1.5 * 2.0 ** 20
RSQRT_SEED = float(0x5F3759DF)
NEWTON_STEPS = 3
RSQRT_OPS = 2 + 3 * NEWTON_STEPS


def build(nc, x, Wq, Wk, Wv, Wb, Wo, ln1, ln2, Wg, Wu, Wd, W8, bias, iscale, wscale, out):
    NB, S, D = x.shape
    H = Wb.shape[1]
    DK = D // H
    F = Wg.shape[1]
    FC = F // P
    T = 32
    NSEG = S // T
    C = 4
    NCH = T // C
    SL = NB * H // P
    LB = P // H
    ST = SL * DK * DK
    TOK = NB * T
    J = TOK // P
    R = P // T
    SCAN_OPS = 4 + C
    HALF = T // 2
    PAIR_ROW = [0] * C
    for delta in range(2, C):
        PAIR_ROW[delta] = PAIR_ROW[delta - 1] + (C - delta + 1) * SL
    PAIRS = PAIR_ROW[C - 1] + SL
    SOLVE_OPS = C * (C - 1)
    assert D == P and F % P == 0 and SL * P == NB * H and TOK == 512 and NSEG % 2 == 0 and FC == 4

    ctx = ExitStack()
    with ctx:
        def sb(name, shape, dt=F32):
            return ctx.enter_context(nc.sbuf_tensor(name, shape, dt))

        def sem(name):
            return ctx.enter_context(nc.semaphore(name))

        wq, wk, wv, wo = (sb(n, [P, D]) for n in ("wq", "wk", "wv", "wo"))
        wb = sb("wb", [P, H])
        wg, wu = sb("wg", [P, F]), sb("wu", [P, F])
        wd = sb("wd", [P, FC, D])
        w8 = sb("w8", [P, D])
        w8t = sb("w8t", [P, D])
        w8part = [sb(f"w8part{i}", [P, D], BF16) for i in range(3)]
        ln1c, ln2c = sb("ln1c", [P, 1]), sb("ln2c", [P, 1])
        isc, wsc, isc_inv = sb("isc", [P, 1]), sb("wsc", [P, 1]), sb("isc_inv", [P, 1])
        bias_b = sb("bias_b", [P, D])
        ident, identh = sb("ident", [P, P]), sb("identh", [P, P], BF16)

        xa = [sb(f"xa{p}", [P, J, D]) for p in range(2)]
        junk = sb("junk", [P, J, D])
        ssx, rx, tx = sb("ssx", [P, J]), sb("rx", [P, J]), sb("tx", [P, 2, J])
        xn = sb("xn", [P, J, D])
        xT = sb("xT", [P, TOK])
        qkvT = sb("qkvT", [P, 3, TOK])
        betaT = sb("betaT", [H, TOK])
        raw = sb("raw", [P, 3, SL, DK, T])
        beta = sb("beta", [P, SL, T])
        sq = sb("sq", [P, 2, SL, DK, T])
        ssqk, rqk, tqk = sb("ssqk", [P, 2, SL, T]), sb("rqk", [P, 2, SL, T]), sb("tqk", [P, 2, 2, SL, T])
        rbeta = sb("rbeta", [P, SL, T])
        wu_rows = [sb(f"wu_rows{p}", [P, T, SL, 2 * DK]) for p in range(2)]
        kb_rows = [sb(f"kb_rows{p}", [P, T, SL, DK]) for p in range(2)]
        qn_rows = [sb(f"qn_rows{p}", [P, T, SL, DK]) for p in range(2)]
        pair_prod = sb("pair_prod", [P, NCH, PAIRS, DK])
        pair = sb("pair", [P, NCH, PAIRS])
        solve_tmp = sb("solve_tmp", [P, NCH, SL, 2 * DK])
        states = sb("states", [P, T, ST])
        ws_prod = sb("ws_prod", [P, C, ST])
        ws = sb("ws", [P, C, SL, DK])
        u2 = sb("u2", [P, C, SL, DK])
        outer = sb("outer", [P, C, ST])
        qs_prod = sb("qs_prod", [P, HALF, ST])
        o_lane = sb("o_lane", [P, SL, DK, T])
        oT = sb("oT", [P, TOK])
        xr = sb("xr", [P, J, D])
        h = sb("h", [P, J, D])
        xh = sb("xh", [P, J, D])
        junk2 = sb("junk2", [P, J, D])
        ssh, rh, th = sb("ssh", [P, J]), sb("rh", [P, J]), sb("th", [P, 2, J])
        y = sb("y", [P, J, D])
        yT = sb("yT", [P, TOK])
        gate = [sb(f"gate{p}", [P, TOK]) for p in range(2)]
        act = sb("act", [P, FC, TOK])
        z = [sb(f"z{p}", [P, J, D]) for p in range(2)]
        zm, ssz, rz, tz, zmr = (sb(n, [P, w]) for n, w in (("zm", J), ("ssz", J), ("rz", J), ("tz", 2 * J), ("zmr", J)))
        junk3 = sb("junk3", [P, J, D])
        w1 = sb("w1", [P, J, D])
        xs = sb("xs", [P, TOK])
        exp_bits = sb("exp_bits", [P, TOK])
        magic = sb("magic", [P, TOK])
        xq = sb("xq", [P, J, D], BF16)
        xqT = sb("xqT", [P, TOK], BF16)
        w1b = sb("w1b", [P, J, D])
        r1 = sb("r1", [P, J, D])
        rm, ssr, rr, tr, rmr = (sb(n, [P, w]) for n, w in (("rm", J), ("ssr", J), ("rr", J), ("tr", 2 * J), ("rmr", J)))
        junk4 = sb("junk4", [P, J, D])
        yout = sb("yout", [P, J, D])

        ps_tp0 = ctx.enter_context(nc.psum_tensor("ps_tp0", [P, 512], F32))
        ps_tp1 = ctx.enter_context(nc.psum_tensor("ps_tp1", [P, 512], F32))
        ps_mm = [ctx.enter_context(nc.psum_tensor(f"ps_mm{i}", [P, 512], F32)) for i in range(4)]
        ps_tk0 = ctx.enter_context(nc.psum_tensor("ps_tk0", [P, 512], F32))
        ps_tk1 = ctx.enter_context(nc.psum_tensor("ps_tk1", [P, 512], F32))

        d_qkv = nc.dram_tensor("d_qkv", (3, NB, H, DK, T), F32, kind="Internal").ap()
        d_beta = nc.dram_tensor("d_beta", (NB, H, T), F32, kind="Internal").ap()
        d_o = nc.dram_tensor("d_o", (NB, H, DK, T), F32, kind="Internal").ap()

        w_in = sem("w_in")
        w_scaled = sem("w_scaled")
        w8_tr = sem("w8_tr")
        ident_ok = sem("ident_ok")
        state_zero = sem("state_zero")
        x_in = [sem(f"x_in{p}") for p in range(2)]
        ssx_ok, rx_ok = sem("ssx_ok"), sem("rx_ok")
        xn_ok, xtr_ok, xT_ok = sem("xn_ok"), sem("xtr_ok"), sem("xT_ok")
        proj_ok = sem("proj_ok")
        qkv_ok = sem("qkv_ok")
        qkv_out, raw_in = sem("qkv_out"), sem("raw_in")
        sq_ok, ucopy_ok = sem("sq_ok"), sem("ucopy_ok")
        ssqk_ok, rqk_ok = sem("ssqk_ok"), sem("rqk_ok")
        rows_ok = sem("rows_ok")
        pprod_ok, pair_ok = sem("pprod_ok"), sem("pair_ok")
        solve_ok = sem("solve_ok")
        scan_ok = sem("scan_ok")
        qs_ok, o_ok = sem("qs_ok"), sem("o_ok")
        o_out, oT_in = sem("o_out"), sem("oT_in")
        xr_in = sem("xr_in")
        wo_ok, h_ok, xh_ok = sem("wo_ok"), sem("h_ok"), sem("xh_ok")
        ssh_ok, rh_ok, y_ok, ytr_ok, yT_ok = (sem(n) for n in ("ssh_ok", "rh_ok", "y_ok", "ytr_ok", "yT_ok"))
        gu_ok, silu_ok, act_ok = sem("gu_ok"), sem("silu_ok"), sem("act_ok")
        wd_ok, z_ok = sem("wd_ok"), sem("z_ok")
        zm_ok = sem("zm_ok")
        ssz_ok, rz_ok = sem("ssz_ok"), sem("rz_ok")
        w1_ok, xs_ok = sem("w1_ok"), sem("xs_ok")
        quant_ok = sem("quant_ok")
        xqtr_ok, xqT_ok, lin_ok, w1b_ok, r1_ok = (sem(n) for n in ("xqtr_ok", "xqT_ok", "lin_ok", "w1b_ok", "r1_ok"))
        rm_ok, ssr_ok, rr_ok = sem("rm_ok"), sem("ssr_ok"), sem("rr_ok")
        yout_ok, y_stored = sem("yout_ok"), sem("y_stored")

        def wait(eng, s, value):
            if not isinstance(value, int) or value > 0:
                eng.wait_ge(s, value)

        def every_segment(eng, body):
            def peeled(s):
                body(s, s % 2, s // 2, lambda d: 0 <= s + d < NSEG)
            for s in range(-2, 3):
                peeled(s)
            with eng.Fori(0, (NSEG - 6) // 2) as m:
                body(m * 2 + 3, 1, m + 1, lambda d: True)
                body(m * 2 + 4, 0, m + 2, lambda d: True)
            for s in range(NSEG - 3, NSEG + 2):
                peeled(s)

        def seg(ap, s):
            return ap[:, bass.ds(s * T, T), :]

        WEIGHTS = 0
        block = ctx.enter_context(nc.Block())

        @block.sync
        def _(sp):
            loads = [(wq[:], Wq), (wk[:], Wk), (wv[:], Wv), (wo[:], Wo), (wb[:], Wb), (wg[:], Wg), (wu[:], Wu),
                     (wd[:], Wd.rearrange("(c p) n -> p c n", p=P)), (w8[:], W8),
                     (ln1c[:], ln1.rearrange("(p a) -> p a", a=1)), (ln2c[:], ln2.rearrange("(p a) -> p a", a=1)),
                     (isc[:], iscale.partition_broadcast(P)), (wsc[:], wscale.partition_broadcast(P)),
                     (bias_b[:], bias.partition_broadcast(P))]
            nonlocal WEIGHTS
            WEIGHTS = 16 * len(loads)

            def load_x(dst, t0, signal):
                for r in range(R):
                    src = x.rearrange("(j r) t d -> r t j d", r=R)[r]
                    sp.dma_start(dst[r * T:(r + 1) * T, :, :], src[bass.ds(t0, T), :, :]).then_inc(signal, 16)

            for dst, src in loads:
                sp.dma_start(dst, src).then_inc(w_in, 16)

            def body(s, par, pair_of, has):
                def reg(value):
                    if not isinstance(value, int):
                        sp.compute_val(value)
                    return value

                t_in, t_out, t_res = (reg((s + d) * T) if has(d) else 0 for d in (2, -2, 0))
                n16, n2, n5, n4, n64 = (reg(v) for v in (s * 16, s * 2, s * 5 + 15, s * 4 + 8, s * 64 + 192))
                n1, m1, p1, p2, m64 = (reg(v) for v in (s, s - 1, s + 1, s + 2, s * 64 + 128))
                if has(2):
                    wait(sp, xn_ok, p1)
                    load_x(xa[par], t_in, x_in[par])
                if has(-1):
                    sp.wait_ge(o_ok, n2)
                    sp.dma_start(d_o.rearrange("(sl b) h v t -> (b h) sl (v t)", sl=SL),
                                 o_lane[:].rearrange("p sl v t -> p sl (v t)")).then_inc(o_out, 16)
                    sp.wait_ge(o_out, n16)
                    wait(sp, wo_ok, m1)
                    sp.dma_start(oT[:].rearrange("p (b t) -> p b t", b=NB),
                                 d_o.rearrange("b h v t -> (h v) b t")).then_inc(oT_in, 16)
                if has(2):
                    sp.wait_ge(qkv_ok, n5)
                    wait(sp, raw_in, m64)
                    for n in range(3):
                        sp.dma_start(d_qkv[n].rearrange("b h d t -> (h d) b t"),
                                     qkvT[:, n, :].rearrange("p (b t) -> p b t", b=NB)).then_inc(qkv_out, 16)
                    sp.dma_start(d_beta.rearrange("b h t -> h b t"),
                                 betaT[:].rearrange("p (b t) -> p b t", b=NB)).then_inc(qkv_out, 16)
                    sp.wait_ge(qkv_out, n64)
                    wait(sp, rows_ok, n4)
                    wait(sp, ucopy_ok, p2)
                    wait(sp, sq_ok, p2)
                    for sl in range(SL):
                        lanes = slice(sl * LB, (sl + 1) * LB)
                        sp.dma_start(raw[:, :, sl, :, :].rearrange("p n d t -> p n (d t)"),
                                     d_qkv[:, lanes].rearrange("n b h d t -> (b h) n (d t)")).then_inc(raw_in, 16)
                        sp.dma_start(beta[:, sl, :], d_beta[lanes].rearrange("b h t -> (b h) t")).then_inc(raw_in, 16)
                if has(-2):
                    sp.wait_ge(yout_ok, m1)
                    for r in range(R):
                        dst = out.rearrange("(j r) t d -> r t j d", r=R)[r]
                        sp.dma_start(dst[bass.ds(t_out, T), :, :],
                                     yout[r * T:(r + 1) * T, :, :]).then_inc(y_stored, 16)
                if has(0):
                    wait(sp, h_ok, n1)
                    wait(sp, xh_ok, n1)
                    load_x(xr, t_res, xr_in)

            every_segment(sp, body)
            sp.wait_ge(y_stored, NSEG * 16 * R)

        @block.tensor
        def _(pe):
            pe.wait_ge(ident_ok, 4)
            pe.wait_ge(w_in, WEIGHTS)
            nc.tensor.transpose(ps_tp1[:, 0:P], w8[:], ident[:]).then_inc(w8_tr, 1)
            pe.wait_ge(w_scaled, 12)

            def project(s, par, has):
                pe.wait_ge(xn_ok, s + 1)
                wait(pe, xT_ok, s)
                for j in range(J):
                    last = nc.tensor.transpose(ps_tp0[:, j * P:(j + 1) * P], xn[:, j, :], ident[:])
                last.then_inc(xtr_ok, 1)
                pe.wait_ge(xT_ok, s + 1)
                wait(pe, qkv_ok, s * 5)
                if has(-3 - 1):
                    pe.wait_ge(silu_ok, (s - 3) * FC)
                    pe.wait_ge(act_ok, (s - 3) * FC)
                for n, w in enumerate((wq, wk, wv)):
                    nc.tensor.matmul(ps_mm[n][:], w[:], xT[:], start=True, stop=True).then_inc(proj_ok, 1)
                nc.tensor.matmul(ps_mm[3][0:H, :], wb[:], xT[:], start=True, stop=True).then_inc(proj_ok, 1)

            def attention_out(s, has):
                pe.wait_ge(oT_in, s * 16 + 16)
                if has(-1):
                    wait(pe, r1_ok, s - 1)
                    pe.wait_ge(h_ok, s)
                for j in range(J):
                    last = nc.tensor.matmul(ps_tk0[:, j * P:(j + 1) * P], oT[:, j * P:(j + 1) * P], wo[:],
                                            start=True, stop=True)
                last.then_inc(wo_ok, 1)

            def mlp(s, has, projected):
                pe.wait_ge(y_ok, s + 1)
                wait(pe, yT_ok, s)
                for j in range(J):
                    last = nc.tensor.transpose(ps_tp1[:, j * P:(j + 1) * P], y[:, j, :], ident[:])
                last.then_inc(ytr_ok, 1)
                pe.wait_ge(yT_ok, s + 1)
                pe.wait_ge(qkv_ok, projected * 5)
                for c in range(FC):
                    wait(pe, silu_ok, s * FC + c - 1)
                    wait(pe, act_ok, s * FC + c - 1)
                    nc.tensor.matmul(ps_mm[2 * c % 4][:], wg[:, c * P:(c + 1) * P], yT[:], start=True, stop=True)
                    nc.tensor.matmul(ps_mm[(2 * c + 1) % 4][:], wu[:, c * P:(c + 1) * P], yT[:],
                                     start=True, stop=True).then_inc(gu_ok, 1)
                pe.wait_ge(act_ok, s * FC + FC)
                wait(pe, z_ok, s)
                for j in range(J):
                    for c in range(FC):
                        last = nc.tensor.matmul(ps_tk1[:, j * P:(j + 1) * P], act[:, c, j * P:(j + 1) * P],
                                                wd[:, c, :], start=(c == 0), stop=(c == FC - 1))
                last.then_inc(wd_ok, 1)

            def linear(s, projected, attended):
                pe.wait_ge(quant_ok, s * 5 + 5)
                wait(pe, xT_ok, projected)
                wait(pe, xqT_ok, s)
                tp = ps_tp0[:, 0:TOK // 2].bitcast(BF16)
                for j in range(J):
                    last = nc.tensor.transpose(tp[:, j * P:(j + 1) * P], xq[:, j, :], identh[:])
                last.then_inc(xqtr_ok, 1)
                pe.wait_ge(xqT_ok, s + 1)
                pe.wait_ge(h_ok, attended)
                wait(pe, r1_ok, s)
                for j in range(J):
                    for i, w in enumerate(w8part):
                        last = nc.tensor.matmul(ps_tk0[:, j * P:(j + 1) * P], xqT[:, j * P:(j + 1) * P], w[:],
                                                start=(i == 0), stop=(i == 2))
                last.then_inc(lin_ok, 1)

            def body(s, par, pair_of, has):
                fixed = isinstance(s, int)
                projected = min(s + 3, NSEG) if fixed else s + 3
                attended = min(s, NSEG) if fixed else s
                if has(-1):
                    attention_out(s - 1, lambda d: has(d - 1))
                if has(2):
                    project(s + 2, par, lambda d: has(d + 2))
                if has(-1):
                    mlp(s - 1, lambda d: has(d - 1), projected)
                if has(-2):
                    linear(s - 2, projected, attended)

            every_segment(pe, body)

        @block.scalar
        def _(act_e):
            act_e.wait_ge(w_in, WEIGHTS)

            def sum_squares(dst, src, junk_t, bias_of=None):
                for j in range(J):
                    b = 0.0 if bias_of is None else bias_of[:, j:j + 1]
                    last = nc.scalar.activation(junk_t[:, j, :], src[:, j, :], ACT.Square, bias=b,
                                                accum_out=dst[:, j:j + 1])
                return last

            def body(s, par, pair_of, has):
                if has(-2):
                    act_e.wait_ge(zm_ok, (s - 2) * 2 + 2)
                    wait(act_e, rz_ok, (s - 2) * (RSQRT_OPS + 1))
                    sum_squares(ssz, z[par], junk3, zm).then_inc(ssz_ok, 1)
                if has(1):
                    n = s + 1
                    act_e.wait_ge(raw_in, n * 64 + 64)
                    wait(act_e, ssqk_ok, n)
                    nc.scalar.activation(sq[:].rearrange("p n s d t -> p (n s d t)"),
                                         raw[:, 0:2].rearrange("p n s d t -> p (n s d t)"),
                                         ACT.Square).then_inc(sq_ok, 1)
                    wait(act_e, scan_ok, (n - 1) * NCH * SCAN_OPS) if has(-1) else None
                    for sl in range(SL):
                        last = nc.scalar.activation(wu_rows[1 - par][:, :, sl, DK:2 * DK],
                                                    raw[:, 2, sl, :, :].rearrange("p d t -> p t d"), ACT.Copy)
                    last.then_inc(ucopy_ok, 1)
                if has(2):
                    n = s + 2
                    act_e.wait_ge(x_in[par], pair_of * (16 * R) + 2 * 16 * R)
                    wait(act_e, rx_ok, n * RSQRT_OPS)
                    sum_squares(ssx, xa[par], junk).then_inc(ssx_ok, 1)
                if has(-2):
                    n = s - 2
                    act_e.wait_ge(rz_ok, (n + 1) * (RSQRT_OPS + 1))
                    wait(act_e, w1b_ok, n)
                    for j in range(J):
                        last = nc.scalar.activation(w1[:, j, :], z[par][:, j, :], ACT.Identity,
                                                    bias=zmr[:, j:j + 1], scale=rz[:, j:j + 1])
                    last.then_inc(w1_ok, 1)
                    act_e.wait_ge(w1_ok, n + 1)
                    wait(act_e, quant_ok, n * 5)
                    nc.scalar.activation(xs[:], w1[:].rearrange("p j d -> p (j d)"), ACT.Copy,
                                         scale=isc_inv[:, 0:1]).then_inc(xs_ok, 1)
                if has(-1):
                    act_e.wait_ge(h_ok, s)
                    wait(act_e, rh_ok, (s - 1) * RSQRT_OPS)
                    sum_squares(ssh, h, junk2).then_inc(ssh_ok, 1)
                if has(2):
                    n = s + 2
                    act_e.wait_ge(rx_ok, (n + 1) * RSQRT_OPS)
                    wait(act_e, xtr_ok, n)
                    for j in range(J):
                        last = nc.scalar.activation(xn[:, j, :], xa[par][:, j, :], ACT.Copy, scale=rx[:, j:j + 1])
                    last.then_inc(xn_ok, 1)
                    act_e.wait_ge(xtr_ok, n + 1)
                    wait(act_e, proj_ok, n * 4)
                    nc.scalar.activation(xT[:], ps_tp0[:], ACT.Copy).then_inc(xT_ok, 1)
                    wait(act_e, qkv_out, n * 64)
                    for i in range(3):
                        act_e.wait_ge(proj_ok, n * 4 + i + 1)
                        nc.scalar.activation(qkvT[:, i, :], ps_mm[i][:], ACT.Silu).then_inc(qkv_ok, 1)
                    act_e.wait_ge(proj_ok, n * 4 + 4)
                    nc.scalar.activation(betaT[:], ps_mm[3][0:H, :], ACT.Tanh, scale=0.5).then_inc(qkv_ok, 1)
                    act_e.wait_ge(qkv_ok, n * 5 + 4)
                    nc.scalar.activation(betaT[:], betaT[:], ACT.Copy, scale=0.5, bias=0.5).then_inc(qkv_ok, 1)
                if has(-1):
                    n = s - 1
                    act_e.wait_ge(rh_ok, (n + 1) * RSQRT_OPS)
                    wait(act_e, ytr_ok, n)
                    for j in range(J):
                        last = nc.scalar.activation(y[:, j, :], h[:, j, :], ACT.Copy, scale=rh[:, j:j + 1])
                    last.then_inc(y_ok, 1)
                    act_e.wait_ge(ytr_ok, n + 1)
                    wait(act_e, gu_ok, n * FC)
                    nc.scalar.activation(yT[:], ps_tp1[:], ACT.Copy).then_inc(yT_ok, 1)
                    for c in range(FC):
                        act_e.wait_ge(gu_ok, n * FC + c + 1)
                        wait(act_e, act_ok, n * FC + c - 1)
                        nc.scalar.activation(gate[c % 2][:], ps_mm[2 * c % 4][:], ACT.Silu).then_inc(silu_ok, 1)
                if has(-2):
                    n = s - 2
                    act_e.wait_ge(xqtr_ok, n + 1)
                    wait(act_e, lin_ok, n)
                    nc.scalar.activation(xqT[:], ps_tp0[:, 0:TOK // 2].bitcast(BF16), ACT.Copy).then_inc(xqT_ok, 1)
                    act_e.wait_ge(rm_ok, n * 2 + 2)
                    wait(act_e, rr_ok, n * (RSQRT_OPS + 1))
                    sum_squares(ssr, r1, junk4, rm).then_inc(ssr_ok, 1)
                    act_e.wait_ge(rr_ok, (n + 1) * (RSQRT_OPS + 1))
                    wait(act_e, y_stored, n * 16 * R)
                    for j in range(J):
                        last = nc.scalar.activation(yout[:, j, :], r1[:, j, :], ACT.Identity,
                                                    bias=rmr[:, j:j + 1], scale=rr[:, j:j + 1])
                    last.then_inc(yout_ok, 1)

            every_segment(act_e, body)

        @block.gpsimd
        def _(pool):
            for m in (ident, identh):
                nc.gpsimd.memset(m[:], 0.0).then_inc(ident_ok, 1)
            pool.wait_ge(ident_ok, 2)
            for m in (ident, identh):
                nc.gpsimd.affine_select(out=m[:], in_=m[:], compare_op=ALU.not_equal, fill=1.0, base=0,
                                        pattern=[[-1, P]], channel_multiplier=1).then_inc(ident_ok, 1)
            pool.wait_ge(w_in, WEIGHTS)

            def prepare(n, par, has):
                wuv, kbv, qnv = wu_rows[par], kb_rows[par], qn_rows[par]
                pool.wait_ge(raw_in, n * 64 + 64)
                pool.wait_ge(rqk_ok, (n + 1) * RSQRT_OPS)
                nc.gpsimd.tensor_tensor(rbeta[:], rqk[:, 1], beta[:], ALU.mult).then_inc(rows_ok, 1)
                if has(-2):
                    pool.wait_ge(scan_ok, (n - 1) * NCH * SCAN_OPS)
                    pool.wait_ge(qs_ok, (n - 1) * 2)

                def scaled(dst, which, r, k):
                    for sl in range(SL):
                        last = nc.gpsimd.tensor_tensor(
                            dst[:, :, sl, 0:DK], raw[:, which, sl].rearrange("p d t -> p t d"),
                            r[:, sl, :].unsqueeze(2).broadcast_to([P, T, DK]), ALU.mult)
                    last.then_inc(rows_ok, 1)

                scaled(wuv, 1, rqk[:, 1], 2)
                scaled(qnv, 0, rqk[:, 0], 3)
                pool.wait_ge(rows_ok, n * 4 + 1)
                scaled(kbv, 1, rbeta, 4)
                pool.wait_ge(rows_ok, n * 4 + 4)
                wait(pool, pair_ok, n)
                wc = wuv[:].rearrange("p (c i) s e -> p c i s e", i=C)
                kc = kbv[:].rearrange("p (c i) s e -> p c i s e", i=C)
                for delta in range(1, C):
                    rows = slice(PAIR_ROW[delta], PAIR_ROW[delta] + (C - delta) * SL)
                    nc.gpsimd.tensor_tensor(
                        pair_prod[:, :, rows, :].rearrange("p c (i s) e -> p c i s e", s=SL),
                        wc[:, :, delta:C, :, 0:DK], kc[:, :, 0:C - delta, :, :], ALU.mult).then_inc(pprod_ok, 1)

            def solve(n, par):
                wc = wu_rows[par][:].rearrange("p (c i) s e -> p c i s e", i=C)
                pool.wait_ge(pair_ok, n + 1)
                pool.wait_ge(ucopy_ok, n + 1)
                k = 0
                for j in range(C - 1):
                    for i in range(j + 1, C):
                        row = PAIR_ROW[i - j] + j * SL
                        coef = pair[:, :, row:row + SL].unsqueeze(3).broadcast_to([P, NCH, SL, 2 * DK])
                        wait(pool, solve_ok, n * SOLVE_OPS + k)
                        nc.gpsimd.tensor_tensor(solve_tmp[:], coef, wc[:, :, j], ALU.mult).then_inc(solve_ok, 1)
                        pool.wait_ge(solve_ok, n * SOLVE_OPS + k + 1)
                        nc.gpsimd.tensor_tensor(wc[:, :, i], wc[:, :, i], solve_tmp[:],
                                                ALU.subtract).then_inc(solve_ok, 1)
                        k += 2

            def read_out(n, par, half):
                t0 = half * HALF
                pool.wait_ge(scan_ok, n * NCH * SCAN_OPS + (half + 1) * (NCH // 2) * SCAN_OPS)
                wait(pool, o_ok, n * 2 + half)
                q = qn_rows[par][:, t0:t0 + HALF].unsqueeze(3).broadcast_to([P, HALF, SL, DK, DK])
                nc.gpsimd.tensor_tensor(qs_prod[:].rearrange("p t (s v k) -> p t s v k", s=SL, v=DK),
                                        states[:, t0:t0 + HALF].rearrange("p t (s v k) -> p t s v k", s=SL, v=DK),
                                        q, ALU.mult).then_inc(qs_ok, 1)

            def body(s, par, pair_of, has):
                if has(1):
                    prepare(s + 1, 1 - par, lambda d: has(d + 1))
                if has(0):
                    read_out(s, par, 0)
                if has(1):
                    solve(s + 1, 1 - par)
                if has(-1):
                    pool.wait_ge(xr_in, s * 16 * R)
                    pool.wait_ge(h_ok, s)
                    wait(pool, z_ok, s - 1)
                    nc.gpsimd.tensor_tensor(xh[:], xr[:], h[:], ALU.add).then_inc(xh_ok, 1)
                if has(-2):
                    pool.wait_ge(w1_ok, s - 1)
                    wait(pool, r1_ok, s - 2)
                    nc.gpsimd.tensor_tensor(w1b[:], w1[:], bias_b[:].unsqueeze(1).broadcast_to([P, J, D]),
                                            ALU.add).then_inc(w1b_ok, 1)
                if has(0):
                    read_out(s, par, 1)

            every_segment(pool, body)

        @block.vector
        def _(dve):
            V = nc.vector
            V.memset(states[:, T - 1, :], 0.0).then_inc(state_zero, 1)
            dve.wait_ge(w_in, WEIGHTS)
            for w, l in ((wq, ln1c), (wk, ln1c), (wv, ln1c), (wb, ln1c), (wg, ln2c), (wu, ln2c)):
                V.tensor_scalar(w[:], w[:], l[:, 0:1], None, ALU.mult).then_inc(w_scaled, 1)
            V.reciprocal(isc_inv[:], isc[:]).then_inc(w_scaled, 1)
            dve.wait_ge(w8_tr, 1)
            V.tensor_scalar(w8t[:], ps_tp1[:, 0:P], wsc[:, 0:1], isc[:, 0:1], ALU.mult, ALU.mult).then_inc(w_scaled, 1)
            dve.wait_ge(w_scaled, 8)
            V.tensor_copy(w8part[0][:], w8t[:]).then_inc(w_scaled, 1)
            dve.wait_ge(w_scaled, 9)
            V.tensor_tensor(w8t[:], w8t[:], w8part[0][:], ALU.subtract).then_inc(w_scaled, 1)
            dve.wait_ge(w_scaled, 10)
            V.tensor_copy(w8part[1][:], w8t[:]).then_inc(w_scaled, 1)
            dve.wait_ge(w_scaled, 11)
            V.tensor_tensor(w8part[2][:], w8t[:], w8part[1][:], ALU.subtract).then_inc(w_scaled, 1)

            def rsqrt(y_, a, t_, ss, scale, eps, signal, base):
                V.tensor_scalar(a, ss, scale, eps, ALU.mult, ALU.add).then_inc(signal, 1)
                dve.wait_ge(signal, base + 1)
                V.tensor_scalar(y_.bitcast(I32), a.bitcast(I32), -0.5, RSQRT_SEED, ALU.mult, ALU.add).then_inc(signal, 1)
                for i in range(NEWTON_STEPS):
                    dve.wait_ge(signal, base + 3 * i + 2)
                    V.tensor_tensor(t_, y_, y_, ALU.mult).then_inc(signal, 1)
                    dve.wait_ge(signal, base + 3 * i + 3)
                    V.scalar_tensor_tensor(out=t_, in0=t_, scalar=-0.5, in1=a, op0=ALU.mult,
                                           op1=ALU.mult).then_inc(signal, 1)
                    dve.wait_ge(signal, base + 3 * i + 4)
                    V.scalar_tensor_tensor(out=y_, in0=t_, scalar=1.5, in1=y_, op0=ALU.add,
                                           op1=ALU.mult).then_inc(signal, 1)

            def flat(t):
                return t[:].rearrange("p j d -> p (j d)")

            def mean(m, src, signal, n):
                V.tensor_reduce(m[:], src[:], AX_X, ALU.add).then_inc(signal, 1)
                dve.wait_ge(signal, n * 2 + 1)
                V.tensor_scalar(m[:], m[:], -1.0 / D, None, ALU.mult).then_inc(signal, 1)

            def norm_scale(r_, t_, ss, m, mr, signal, n):
                base = n * (RSQRT_OPS + 1)
                rsqrt(r_[:], t_[:, 0:J], t_[:, J:2 * J], ss[:], 1.0 / D, LN_EPS, signal, base)
                dve.wait_ge(signal, base + RSQRT_OPS)
                V.tensor_tensor(mr[:], m[:], r_[:], ALU.mult).then_inc(signal, 1)

            def chunk(s, par, c, first):
                base = s * (NCH * SCAN_OPS) + c * SCAN_OPS
                prev = (c * C - 1) % T
                t0 = c * C
                if first:
                    dve.wait_ge(state_zero, 1)
                else:
                    dve.wait_ge(scan_ok, base)
                if c == 0:
                    dve.wait_ge(solve_ok, (s + 1) * SOLVE_OPS)
                w_ = wu_rows[par][:, t0:t0 + C, :, 0:DK].unsqueeze(3).broadcast_to([P, C, SL, DK, DK])
                s_ = states[:, prev, :].rearrange("p (s v k) -> p s v k", s=SL, v=DK)
                V.tensor_tensor(ws_prod[:].rearrange("p c (s v k) -> p c s v k", s=SL, v=DK), w_,
                                s_.unsqueeze(1).broadcast_to([P, C, SL, DK, DK]), ALU.mult).then_inc(scan_ok, 1)
                dve.wait_ge(scan_ok, base + 1)
                V.tensor_reduce(ws[:], ws_prod[:].rearrange("p c (s v k) -> p c s v k", s=SL, v=DK), AX_X,
                                ALU.add).then_inc(scan_ok, 1)
                dve.wait_ge(scan_ok, base + 2)
                V.tensor_tensor(u2[:], wu_rows[par][:, t0:t0 + C, :, DK:2 * DK], ws[:], ALU.subtract).then_inc(scan_ok, 1)
                dve.wait_ge(scan_ok, base + 3)
                V.tensor_tensor(outer[:].rearrange("p c (s v k) -> p c s v k", s=SL, v=DK),
                                u2[:].unsqueeze(4).broadcast_to([P, C, SL, DK, DK]),
                                kb_rows[par][:, t0:t0 + C].unsqueeze(3).broadcast_to([P, C, SL, DK, DK]),
                                ALU.mult).then_inc(scan_ok, 1)
                for i in range(C):
                    if i == 0 and c % (NCH // 2) == 0:
                        wait(dve, qs_ok, (s - 1) * 2 + c // (NCH // 2) + 1)
                    dve.wait_ge(scan_ok, base + 4 + i)
                    V.tensor_tensor(states[:, t0 + i, :], states[:, (t0 + i - 1) % T, :], outer[:, i, :],
                                    ALU.add).then_inc(scan_ok, 1)

            def sum_read_out(n, half):
                dve.wait_ge(qs_ok, n * 2 + half + 1)
                if half == 0:
                    wait(dve, o_out, n * 16)
                t0 = half * HALF
                V.tensor_reduce(o_lane[:, :, :, t0:t0 + HALF].rearrange("p s v t -> p t s v"),
                                qs_prod[:].rearrange("p t (s v k) -> p t s v k", s=SL, v=DK), AX_X,
                                ALU.add).then_inc(o_ok, 1)

            def body(s, par, pair_of, has):
                def step(c):
                    if has(0):
                        chunk(s, par, c, first=(isinstance(s, int) and s == 0 and c == 0))

                if has(-1):
                    sum_read_out(s - 1, 1)
                if has(-2):
                    n = s - 2
                    dve.wait_ge(z_ok, n + 1)
                    wait(dve, ssz_ok, n)
                    mean(zm, z[par], zm_ok, n)
                step(0)
                if has(1):
                    n = s + 1
                    dve.wait_ge(sq_ok, n + 1)
                    wait(dve, rows_ok, n * 4)
                    V.tensor_reduce(ssqk[:].rearrange("p n s t -> p (n s) t"),
                                    sq[:].rearrange("p n s d t -> p (n s) t d"), AX_X, ALU.add).then_inc(ssqk_ok, 1)
                step(1)
                if has(1):
                    dve.wait_ge(ssqk_ok, s + 2)
                    rsqrt(rqk[:].rearrange("p n s t -> p (n s t)"), tqk[:, 0].rearrange("p n s t -> p (n s t)"),
                          tqk[:, 1].rearrange("p n s t -> p (n s t)"), ssqk[:].rearrange("p n s t -> p (n s t)"),
                          1.0, RMS_EPS, rqk_ok, (s + 1) * RSQRT_OPS)
                if has(-2):
                    n = s - 2
                    dve.wait_ge(ssz_ok, n + 1)
                    wait(dve, w1_ok, n)
                    norm_scale(rz, tz, ssz, zm, zmr, rz_ok, n)
                step(2)
                if has(2):
                    n = s + 2
                    dve.wait_ge(ssx_ok, n + 1)
                    wait(dve, xn_ok, n)
                    rsqrt(rx[:], tx[:, 0], tx[:, 1], ssx[:], 1.0 / D, RMS_EPS, rx_ok, n * RSQRT_OPS)
                if has(-1):
                    n = s - 1
                    dve.wait_ge(wo_ok, n + 1)
                    dve.wait_ge(xr_in, (n + 1) * 16 * R)
                    wait(dve, y_ok, n)
                    wait(dve, xh_ok, n)
                    V.tensor_tensor(flat(h), ps_tk0[:], flat(xr), ALU.add).then_inc(h_ok, 1)
                step(3)
                if has(1):
                    n = s + 1
                    dve.wait_ge(pprod_ok, (n + 1) * (C - 1))
                    wait(dve, solve_ok, n * SOLVE_OPS)
                    V.tensor_reduce(pair[:], pair_prod[:], AX_X, ALU.add).then_inc(pair_ok, 1)
                if has(-1):
                    n = s - 1
                    dve.wait_ge(ssh_ok, n + 1)
                    wait(dve, y_ok, n)
                    rsqrt(rh[:], th[:, 0], th[:, 1], ssh[:], 1.0 / D, RMS_EPS, rh_ok, n * RSQRT_OPS)
                if has(-2):
                    n = s - 2
                    base = n * 5
                    dve.wait_ge(xs_ok, n + 1)
                    V.tensor_scalar(xs[:], xs[:], FP8_MAX, -FP8_MAX, ALU.min, ALU.max).then_inc(quant_ok, 1)
                    dve.wait_ge(quant_ok, base + 1)
                    V.tensor_scalar(exp_bits[:].bitcast(I32), xs[:].bitcast(I32), EXPONENT_BITS, None,
                                    ALU.bitwise_and).then_inc(quant_ok, 1)
                    dve.wait_ge(quant_ok, base + 2)
                    V.tensor_scalar(magic[:], exp_bits[:], FP8_MIN_NORMAL, ROUND_TO_4_BITS, ALU.max,
                                    ALU.mult).then_inc(quant_ok, 1)
                    dve.wait_ge(quant_ok, base + 3)
                    V.tensor_tensor(xs[:], xs[:], magic[:], ALU.add).then_inc(quant_ok, 1)
                    dve.wait_ge(quant_ok, base + 4)
                    wait(dve, xqtr_ok, n)
                    V.tensor_tensor(flat(xq), xs[:], magic[:], ALU.subtract).then_inc(quant_ok, 1)
                step(4)
                if has(0):
                    sum_read_out(s, 0)
                step(5)
                if has(-1):
                    n = s - 1
                    for c in range(FC):
                        dve.wait_ge(silu_ok, n * FC + c + 1)
                        if c == 0:
                            wait(dve, wd_ok, n)
                        V.tensor_tensor(act[:, c, :], gate[c % 2][:], ps_mm[(2 * c + 1) % 4][:],
                                        ALU.mult).then_inc(act_ok, 1)
                step(6)
                if has(-1):
                    n = s - 1
                    dve.wait_ge(wd_ok, n + 1)
                    dve.wait_ge(xh_ok, n + 1)
                    if has(-3):
                        wait(dve, w1_ok, n - 1)
                    V.tensor_tensor(flat(z[1 - par]), ps_tk1[:], flat(xh), ALU.add).then_inc(z_ok, 1)
                if has(-2):
                    n = s - 2
                    dve.wait_ge(lin_ok, n + 1)
                    dve.wait_ge(w1b_ok, n + 1)
                    wait(dve, yout_ok, n)
                    V.tensor_tensor(flat(r1), ps_tk0[:], flat(w1b), ALU.add).then_inc(r1_ok, 1)
                    dve.wait_ge(r1_ok, n + 1)
                    wait(dve, ssr_ok, n)
                    mean(rm, r1, rm_ok, n)
                step(7)
                if has(-2):
                    n = s - 2
                    dve.wait_ge(ssr_ok, n + 1)
                    wait(dve, yout_ok, n)
                    norm_scale(rr, tr, ssr, rm, rmr, rr_ok, n)

            every_segment(dve, body)


_INS = ["L0_attn_hidden_states", "L0_attn_Wq", "L0_attn_Wk", "L0_attn_Wv", "L0_attn_Wb", "L0_attn_Wo", "L0_attn_ln1",
        "L0_attn_ln2", "L0_attn_Wg", "L0_attn_Wu", "L0_attn_Wd", "L0_ffn_weight_fp8", "L0_ffn_bias",
        "L0_ffn_input_scale", "L0_ffn_weight_scale"]


def kernel(**inputs):
    import numpy as _np
    import concourse.bacc as _bacc
    from concourse import mybir as _mybir
    from concourse.bass_utils import run_bass_kernel_spmd as _run

    nc = _bacc.Bacc("TRN2", target_bir_lowering=False, num_devices=1)
    arrays, args = {}, []
    for name in _INS:
        a = _np.ascontiguousarray(inputs[name])
        arrays[f"in_{name}"] = a
        args.append(nc.dram_tensor(f"in_{name}", a.shape, _mybir.dt.from_np(a.dtype), kind="ExternalInput").ap())
    shape = inputs[_INS[0]].shape
    result = nc.dram_tensor("out_0", shape, _mybir.dt.float32, kind="ExternalOutput").ap()
    build(nc, *args, result)
    r = _run(nc, [arrays], core_ids=[0])
    return r.results[0]["out_0"]
```

```python
from contextlib import ExitStack

import concourse.bass as bass
from concourse import mybir

P = 128
F32 = mybir.dt.float32
BF16 = mybir.dt.bfloat16
I32 = mybir.dt.int32
ALU = mybir.AluOpType
ACT = mybir.ActivationFunctionType
AX_X = mybir.AxisListType.X

RMS_EPS = 1e-6
LN_EPS = 1e-5
FP8_MAX = 448.0
FP8_MIN_NORMAL = 2.0 ** -6
EXPONENT_BITS = 0x7F800000
ROUND_TO_4_BITS = 1.5 * 2.0 ** 20
RSQRT_SEED = float(0x5F3759DF)
NEWTON_STEPS = 3
NORM_OPS = 3 + 3 * NEWTON_STEPS
NORM_SLOTS = (7, 8, 9, 10, 11, 12, 13, 14, 15, 16, 17, 18)
QUANT_SLOTS = (31, 32, 33, 34, 35)
GATED_SLOTS = (29, 39, 41, 45)
PAIR_SLOT, H_SLOT, R_SLOT, Z_SLOT = 30, 39, 49, 55


def build(nc, x, Wq, Wk, Wv, Wb, Wo, ln1, ln2, Wg, Wu, Wd, W8, bias, iscale, wscale, out):
    NB, S, D = x.shape
    H = Wb.shape[1]
    DK = D // H
    F = Wg.shape[1]
    FC = F // P
    T = 32
    NSEG = S // T
    C = 4
    NCH = T // C
    SL = NB * H // P
    LB = P // H
    ST = SL * DK * DK
    TOK = NB * T
    J = TOK // P
    R = P // T
    HALF = T // 2
    SCAN_OPS = 3 + C
    SEG_OPS = NCH * SCAN_OPS
    PAIR_ROW = [0] * C
    for delta in range(2, C):
        PAIR_ROW[delta] = PAIR_ROW[delta - 1] + (C - delta + 1) * SL
    PAIRS = PAIR_ROW[C - 1] + SL
    SOLVE_OPS = C * (C - 1)
    QK = 2 * SL * T
    COL_X, COL_H, COL_Z, COL_R, COLS = (QK + i * J for i in range(5))
    LANE_DMAS = 16 * 3 * SL
    OUT_DMAS = 16 * 6
    assert D == P and F % P == 0 and SL * P == NB * H and TOK == 512 and FC == 4 and NCH == 8

    ctx = ExitStack()
    with ctx:
        def sb(name, shape, dt=F32):
            return ctx.enter_context(nc.sbuf_tensor(name, shape, dt))

        def psum(name):
            return ctx.enter_context(nc.psum_tensor(name, [P, 512], F32))

        def sem(name):
            return ctx.enter_context(nc.semaphore(name))

        wq, wk, wv, wo = (sb(n, [P, D]) for n in ("wq", "wk", "wv", "wo"))
        wb = sb("wb", [P, H])
        wg, wu = sb("wg", [P, F]), sb("wu", [P, F])
        wd = sb("wd", [P, FC, D])
        w8 = sb("w8", [P, D])
        w8t = sb("w8t", [P, D])
        w8part = [sb(f"w8part{i}", [P, D], BF16) for i in range(3)]
        ln1c, ln2c = sb("ln1c", [P, 1]), sb("ln2c", [P, 1])
        isc, wsc, isc_inv = sb("isc", [P, 1]), sb("wsc", [P, 1]), sb("isc_inv", [P, 1])
        bias_b = sb("bias_b", [P, D])
        ident, identh = sb("ident", [P, P]), sb("identh", [P, P], BF16)
        head_sum = sb("head_sum", [P, 2 * H])

        sumsq, eps, radicand, rs, newton = (sb(n, [P, COLS]) for n in ("sumsq", "eps", "radicand", "rs", "newton"))
        nmean, nmean_rs = sb("nmean", [P, 2 * J]), sb("nmean_rs", [P, 2 * J])
        rs_qk = rs[:, 0:QK].rearrange("p (n s t) -> p n s t", n=2, s=SL)
        rs_x, rs_h, rs_z, rs_r = (rs[:, c:c + J] for c in (COL_X, COL_H, COL_Z, COL_R))
        xa = [sb(f"xa{p}", [P, J, D]) for p in range(2)]
        xx = sb("xx", [P, J, D], BF16)
        xn = sb("xn", [P, J, D])
        xT = sb("xT", [P, TOK])
        qkvT = sb("qkvT", [P, 3, TOK])
        betaT = sb("betaT", [H, TOK])
        sqT = sb("sqT", [P, 2, TOK])
        ssT = sb("ssT", [P, TOK])
        raw = sb("raw", [P, 3, SL, DK, T])
        beta = sb("beta", [P, SL, T])
        rbeta = sb("rbeta", [P, SL, T])
        wu_rows = [sb(f"wu_rows{p}", [P, T, SL, 2 * DK]) for p in range(2)]
        kb_rows = [sb(f"kb_rows{p}", [P, T, SL, DK]) for p in range(2)]
        qn_rows = [sb(f"qn_rows{p}", [P, T, SL, DK]) for p in range(2)]
        pair_prod = sb("pair_prod", [P, NCH, PAIRS, DK])
        pair = sb("pair", [P, NCH, PAIRS])
        solve_tmp = sb("solve_tmp", [P, NCH, SL, 2 * DK])
        states = sb("states", [P, T, ST])
        ws_prod = [sb(f"ws_prod{p}", [P, T, SL, DK, DK + 1]) for p in range(2)]
        nu = sb("nu", [P, C, SL, DK])
        outer = sb("outer", [P, C, ST])
        qs_prod = [sb(f"qs_prod{i}", [P, DK, HALF * SL * DK]) for i in range(2)]
        o_lane = sb("o_lane", [P, SL, DK, T])
        oT = sb("oT", [P, TOK])
        xr = sb("xr", [P, J, D])
        h = sb("h", [P, J, D])
        hh = sb("hh", [P, J, D], BF16)
        xh = sb("xh", [P, J, D])
        y = sb("y", [P, J, D])
        yT = sb("yT", [P, TOK])
        gate = [sb(f"gate{p}", [P, TOK]) for p in range(2)]
        act = sb("act", [P, FC, TOK])
        z = sb("z", [P, J, D])
        zz = sb("zz", [P, 2, J, D], BF16)
        w1 = sb("w1", [P, J, D])
        xs = sb("xs", [P, TOK])
        magic = sb("magic", [P, TOK])
        xq = sb("xq", [P, J, D], BF16)
        xqT = sb("xqT", [P, TOK], BF16)
        w1b = sb("w1b", [P, J, D])
        r1 = sb("r1", [P, J, D])
        rr = sb("rr", [P, 2, J, D], BF16)
        yout = sb("yout", [P, J, D])

        ps_x = psum("ps_x")
        ps_p = psum("ps_p")
        ps_oq = psum("ps_oq")
        ps_g = [psum(f"ps_g{i}") for i in range(3)]
        ps_h = psum("ps_h")
        ps_z = psum("ps_z")
        ps_q = ps_oq[:, 0:TOK // 2].bitcast(BF16)
        ps_o = ps_oq[:, TOK // 2:TOK]

        d_qkv = nc.dram_tensor("d_qkv", (3, NB, H, DK, T), F32, kind="Internal").ap()
        d_stat = nc.dram_tensor("d_stat", (3, NB, H, T), F32, kind="Internal").ap()
        d_o = nc.dram_tensor("d_o", (NB, H, DK, T), F32, kind="Internal").ap()

        w_in, w_scaled, w8_tr = sem("w_in"), sem("w_scaled"), sem("w8_tr")
        const_ok, init_ok = sem("const_ok"), sem("init_ok")
        norm_ok = sem("norm_ok")
        x_in = [sem(f"x_in{p}") for p in range(2)]
        ssx_ok, xn_ok, xtr_ok, xT_ok = (sem(n) for n in ("ssx_ok", "xn_ok", "xtr_ok", "xT_ok"))
        proj_ok = sem("proj_ok")
        qkv_ok = sem("qkv_ok")
        sqT_ok, ssp_ok, ssT_ok = sem("sqT_ok"), sem("ssp_ok"), sem("ssT_ok")
        qkv_out, raw_in = sem("qkv_out"), sem("raw_in")
        v_ok = sem("v_ok")
        rows_ok = sem("rows_ok")
        pprod_ok, pair_ok = sem("pprod_ok"), sem("pair_ok")
        solve_ok, u_ok = sem("solve_ok"), sem("u_ok")
        scan_ok = sem("scan_ok")
        qs_ok, osum_ok, o_ok = sem("qs_ok"), sem("osum_ok"), sem("o_ok")
        o_out, oT_in = sem("o_out"), sem("oT_in")
        xr_in = sem("xr_in")
        wo_ok, h_ok, ssh_ok, xh_ok = (sem(n) for n in ("wo_ok", "h_ok", "ssh_ok", "xh_ok"))
        y_ok, ytr_ok, yT_ok = (sem(n) for n in ("y_ok", "ytr_ok", "yT_ok"))
        gu_ok, silu_ok, act_ok = sem("gu_ok"), sem("silu_ok"), sem("act_ok")
        wd_ok, z_ok, zmean_ok, ssz_ok = (sem(n) for n in ("wd_ok", "z_ok", "zmean_ok", "ssz_ok"))
        w1_ok, xs_ok = sem("w1_ok"), sem("xs_ok")
        quant_ok = sem("quant_ok")
        xqtr_ok, xqT_ok, lin_ok, w1b_ok = (sem(n) for n in ("xqtr_ok", "xqT_ok", "lin_ok", "w1b_ok"))
        r_ok, rmean_ok, ssr_ok = sem("r_ok"), sem("rmean_ok"), sem("ssr_ok")
        yout_ok, y_stored = sem("yout_ok"), sem("y_stored")

        def wait(eng, s, value):
            if not isinstance(value, int) or value > 0:
                eng.wait_ge(s, value)

        def done(v):
            return max(0, min(v, NSEG)) if isinstance(v, int) else v

        FIRST, LAST = -3, NSEG + 3
        LOOP_FROM, LOOP_PAIRS = 5, (NSEG - 8) // 2

        def is_first(s):
            return isinstance(s, int) and s == FIRST

        def every_iteration(eng, body):
            def peeled(s):
                body(s, s % 2, s // 2, lambda d: 0 <= s + d < NSEG)
            for s in range(FIRST, LOOP_FROM):
                peeled(s)
            with eng.Fori(0, LOOP_PAIRS) as m:
                body(m * 2 + LOOP_FROM, 1, m + LOOP_FROM // 2, lambda d: True)
                body(m * 2 + LOOP_FROM + 1, 0, m + LOOP_FROM // 2 + 1, lambda d: True)
            for s in range(LOOP_FROM + 2 * LOOP_PAIRS, LAST + 1):
                peeled(s)

        block = ctx.enter_context(nc.Block())
        loads = [(wq[:], Wq), (wk[:], Wk), (wv[:], Wv), (wb[:], Wb), (ln1c[:], ln1.rearrange("(p a) -> p a", a=1)),
                 (wo[:], Wo), (wg[:], Wg), (wu[:], Wu), (wd[:], Wd.rearrange("(c p) n -> p c n", p=P)), (w8[:], W8),
                 (ln2c[:], ln2.rearrange("(p a) -> p a", a=1)), (isc[:], iscale.partition_broadcast(P)),
                 (wsc[:], wscale.partition_broadcast(P)), (bias_b[:], bias.partition_broadcast(P))]
        WEIGHTS = 16 * len(loads)

        @block.sync
        def _(sp):
            def load_x(dst, t0, signal):
                for r in range(R):
                    src = x.rearrange("(j r) t d -> r t j d", r=R)[r]
                    sp.dma_start(dst[r * T:(r + 1) * T, :, :], src[bass.ds(t0, T), :, :]).then_inc(signal, 16)

            def body(s, par, pair_of, has):
                def reg(value):
                    if not isinstance(value, int):
                        sp.compute_val(value)
                    return value

                t_in, t_out, t_res = (reg((s + d) * T) if has(d) else 0 for d in (3, -4, -1))
                a_xn, a_o, a_oout, a_wo, a_qkv, a_st, a_raw, a_out, a_rows, a_v, a_h, a_y, a_norm = (reg(v) for v in (
                    done(s + 2), done(s) * 2, done(s) * 16, done(s - 1), (s + 3) * 5, s + 3, (s + 2) * LANE_DMAS,
                    (s + 3) * OUT_DMAS, done(s + 2) * 4, done(s + 2), done(s - 1), done(s - 3), (s + 2) * NORM_OPS + 1))
                if has(3):
                    wait(sp, xn_ok, a_xn)
                    load_x(xa[1 - par], t_in, x_in[1 - par])
                if is_first(s):
                    for dst, src in loads:
                        sp.dma_start(dst, src).then_inc(w_in, 16)
                if has(-1):
                    wait(sp, h_ok, a_h)
                    wait(sp, xh_ok, a_h)
                    load_x(xr, t_res, xr_in)
                if has(-1):
                    sp.wait_ge(o_ok, a_o)
                    sp.dma_start(d_o.rearrange("(sl b) h v t -> (b h) sl (v t)", sl=SL),
                                 o_lane[:].rearrange("p sl v t -> p sl (v t)")).then_inc(o_out, 16)
                if has(-1):
                    sp.wait_ge(o_out, a_oout)
                    wait(sp, wo_ok, a_wo)
                    sp.dma_start(oT[:].rearrange("p (b t) -> p b t", b=NB),
                                 d_o.rearrange("b h v t -> (h v) b t")).then_inc(oT_in, 16)
                if has(-4):
                    sp.wait_ge(yout_ok, a_y)
                    for r in range(R):
                        dst = out.rearrange("(j r) t d -> r t j d", r=R)[r]
                        sp.dma_start(dst[bass.ds(t_out, T), :, :],
                                     yout[r * T:(r + 1) * T, :, :]).then_inc(y_stored, 16)
                if has(2):
                    sp.wait_ge(qkv_ok, a_qkv)
                    wait(sp, raw_in, a_raw)
                    for n in range(3):
                        sp.dma_start(d_qkv[n].rearrange("b h d t -> (h d) b t"),
                                     qkvT[:, n, :].rearrange("p (b t) -> p b t", b=NB)).then_inc(qkv_out, 16)
                    sp.dma_start(d_stat[0].rearrange("b h t -> h b t"),
                                 betaT[:].rearrange("p (b t) -> p b t", b=NB)).then_inc(qkv_out, 16)
                if has(2):
                    sp.wait_ge(ssT_ok, a_st)
                    wait(sp, raw_in, a_raw)
                    for n in range(2):
                        row = P // 2 + n * 2 * H
                        sp.dma_start(d_stat[1 + n].rearrange("b h t -> h b t"),
                                     ssT[row:row + H, :].rearrange("p (b t) -> p b t", b=NB)).then_inc(qkv_out, 16)
                if has(2):
                    sp.wait_ge(qkv_out, a_out)
                    wait(sp, rows_ok, a_rows)
                    wait(sp, v_ok, a_v)
                    wait(sp, norm_ok, a_norm)
                    for sl in range(SL):
                        lanes = slice(sl * LB, (sl + 1) * LB)
                        sp.dma_start(sumsq[:, 0:QK].rearrange("p (n s t) -> p n s t", n=2, s=SL)[:, :, sl, :],
                                     d_stat[1:3, lanes].rearrange("n b h t -> (b h) n t")).then_inc(raw_in, 16)
                        sp.dma_start(beta[:, sl, :],
                                     d_stat[0, lanes].rearrange("b h t -> (b h) t")).then_inc(raw_in, 16)
                        sp.dma_start(raw[:, :, sl, :, :].rearrange("p n d t -> p n (d t)"),
                                     d_qkv[:, lanes].rearrange("n b h d t -> (b h) n (d t)")).then_inc(raw_in, 16)

            every_iteration(sp, body)
            sp.wait_ge(y_stored, NSEG * 16 * R)

        @block.tensor
        def _(pe):
            mm = nc.tensor.matmul

            def transposes(dst, src, identity, signal):
                for j in range(J):
                    last = nc.tensor.transpose(dst[:, j * P:(j + 1) * P], src[:, j, :], identity[:])
                last.then_inc(signal, 1)

            def sum_read_out(n, half):
                pe.wait_ge(qs_ok, n * 2 + half + 1)
                wait(pe, o_ok, n * 2 + half)
                for k in range(DK):
                    last = mm(ps_o, ident[:], qs_prod[half][:, k, :], start=(k == 0), stop=(k == DK - 1))
                last.then_inc(osum_ok, 1)

            def gate_up(n, c):
                if c == 0:
                    pe.wait_ge(yT_ok, n + 1)
                    wait(pe, act_ok, n * FC)
                for i, w in ((2 * c, wg), (2 * c + 1, wu)):
                    if i >= 3 and i % 2:
                        pe.wait_ge(silu_ok, n * FC + (i - 3) // 2 + 1)
                    elif i >= 3:
                        pe.wait_ge(act_ok, n * FC + (i - 3) // 2 + 1)
                    last = mm(ps_g[i % 3][:], w[:, c * P:(c + 1) * P], yT[:], start=True, stop=True)
                last.then_inc(gu_ok, 1)

            def project(n, i):
                w = (wq, wk, wv, wb)[i]
                if i == 0:
                    pe.wait_ge(xT_ok, n + 1)
                    wait(pe, qkv_ok, n * 5)
                elif i >= 2:
                    pe.wait_ge(qkv_ok, n * 5 + i - 1)
                mm((ps_p, ps_x)[i % 2][0:w.shape[1], :], w[:], xT[:], start=True, stop=True).then_inc(proj_ok, 1)

            def attention_out(n, read):
                pe.wait_ge(oT_in, n * 16 + 16)
                wait(pe, r_ok, read)
                for j in range(J):
                    last = mm(ps_h[:, j * P:(j + 1) * P], oT[:, j * P:(j + 1) * P], wo[:], start=True, stop=True)
                last.then_inc(wo_ok, 1)

            def sum_heads(n):
                pe.wait_ge(sqT_ok, n + 1)
                pe.wait_ge(qkv_ok, n * 5 + 2)
                for i in range(2):
                    row = P // 2 + i * 2 * H
                    last = mm(ps_x[row:row + 2 * H, :], head_sum[:], sqT[:, i, :], start=True, stop=True)
                last.then_inc(ssp_ok, 1)

            def linear(n, read):
                pe.wait_ge(xqT_ok, n + 1)
                wait(pe, h_ok, read)
                for j in range(J):
                    for i, w in enumerate(w8part):
                        last = mm(ps_h[:, j * P:(j + 1) * P], xqT[:, j * P:(j + 1) * P], w[:],
                                  start=(i == 0), stop=(i == 2))
                last.then_inc(lin_ok, 1)

            def down(n):
                pe.wait_ge(act_ok, n * FC + FC)
                for j in range(J):
                    for c in range(FC):
                        last = mm(ps_z[:, j * P:(j + 1) * P], act[:, c, j * P:(j + 1) * P], wd[:, c, :],
                                  start=(c == 0), stop=(c == FC - 1))
                last.then_inc(wd_ok, 1)

            pe.wait_ge(const_ok, 8)
            pe.wait_ge(w_in, WEIGHTS)
            nc.tensor.transpose(ps_z[:, 0:P], w8[:], ident[:]).then_inc(w8_tr, 1)
            pe.wait_ge(w_scaled, 12)

            def body(s, par, pair_of, has):
                if has(-1):
                    sum_read_out(s - 1, 0)
                if has(-1):
                    sum_read_out(s - 1, 1)
                if has(-2):
                    pe.wait_ge(y_ok, s - 1)
                    wait(pe, z_ok, s - 2)
                    transposes(ps_z, y, ident, ytr_ok)
                if has(2):
                    pe.wait_ge(xn_ok, s + 3)
                    wait(pe, qkv_ok, (s + 2) * 5)
                    wait(pe, ssT_ok, s + 2)
                    transposes(ps_x, xn, ident, xtr_ok)
                if has(-2):
                    gate_up(s - 2, 0)
                if has(2):
                    project(s + 2, 0)
                if has(2):
                    project(s + 2, 1)
                if has(-2):
                    gate_up(s - 2, 1)
                if has(2):
                    project(s + 2, 2)
                if has(-1):
                    attention_out(s - 1, done(s - 3))
                if has(2):
                    project(s + 2, 3)
                if has(-2):
                    gate_up(s - 2, 2)
                if has(2):
                    sum_heads(s + 2)
                if has(-3):
                    pe.wait_ge(quant_ok, (s - 3) * 5 + 5)
                    wait(pe, xqT_ok, s - 3)
                    transposes(ps_q, xq, identh, xqtr_ok)
                if has(-2):
                    gate_up(s - 2, 3)
                if has(-3):
                    linear(s - 3, done(s))
                if has(-2):
                    down(s - 2)

            every_iteration(pe, body)

        @block.scalar
        def _(sc):
            activation = nc.scalar.activation
            RMS = float(D) ** -0.5

            def tiles(func, dst, src, accum=None, bias_of=None, scale_of=None, scale=1.0):
                for j in range(J):
                    more = {} if accum is None else {"accum_out": accum[:, j:j + 1]}
                    if bias_of is not None:
                        more["bias"] = bias_of[:, j:j + 1]
                    last = activation(dst[:, j, :], src[:, j, :], func,
                                      scale=scale if scale_of is None else scale_of[:, j:j + 1], **more)
                return last

            def copy_sums(n, half):
                sc.wait_ge(osum_ok, n * 2 + half + 1)
                if half == 0:
                    wait(sc, o_out, n * 16)
                t0 = half * HALF
                activation(o_lane[:, :, :, t0:t0 + HALF].rearrange("p s v t -> p t (s v)"),
                           ps_o.rearrange("p (t e) -> p t e", t=HALF), ACT.Copy).then_inc(o_ok, 1)

            def silu_gate(n, c):
                sc.wait_ge(gu_ok, n * FC + c + 1)
                wait(sc, act_ok, n * FC + c - 1)
                activation(gate[c % 2][:], ps_g[2 * c % 3][:], ACT.Silu).then_inc(silu_ok, 1)

            sc.wait_ge(init_ok, 4)

            def silu_projection(n, i):
                if i == 0:
                    wait(sc, qkv_out, n * OUT_DMAS)
                sc.wait_ge(proj_ok, n * 4 + i + 1)
                activation(qkvT[:, i, :], (ps_p, ps_x)[i % 2][:], ACT.Silu).then_inc(qkv_ok, 1)

            def body(s, par, pair_of, has):
                if has(1):
                    n = s + 1
                    sc.wait_ge(raw_in, (n + 1) * LANE_DMAS)
                    wait(sc, scan_ok, done(s) * SEG_OPS)
                    wait(sc, u_ok, done(s))
                    for sl in range(SL):
                        last = activation(wu_rows[1 - par][:, :, sl, DK:2 * DK],
                                          raw[:, 2, sl, :, :].rearrange("p d t -> p t d"), ACT.Copy, scale=-1.0)
                    last.then_inc(v_ok, 1)
                if has(-1):
                    copy_sums(s - 1, 0)
                if has(-1):
                    copy_sums(s - 1, 1)
                if has(-2):
                    sc.wait_ge(norm_ok, (s + 3) * NORM_OPS)
                    wait(sc, ytr_ok, s - 2)
                    tiles(ACT.Copy, y, h, scale_of=rs_h).then_inc(y_ok, 1)
                if has(2):
                    sc.wait_ge(norm_ok, (s + 3) * NORM_OPS)
                    wait(sc, xtr_ok, s + 2)
                    tiles(ACT.Copy, xn, xa[par], scale_of=rs_x).then_inc(xn_ok, 1)
                if has(-2):
                    sc.wait_ge(ytr_ok, s - 1)
                    wait(sc, gu_ok, (s - 2) * FC)
                    activation(yT[:], ps_z[:], ACT.Copy).then_inc(yT_ok, 1)
                if has(-3):
                    sc.wait_ge(norm_ok, (s + 3) * NORM_OPS)
                    wait(sc, w1b_ok, s - 3)
                    tiles(ACT.Identity, w1, z, scale_of=rs_z, bias_of=nmean_rs[:, 0:J]).then_inc(w1_ok, 1)
                if has(2):
                    sc.wait_ge(xtr_ok, s + 3)
                    wait(sc, proj_ok, (s + 2) * 4)
                    activation(xT[:], ps_x[:], ACT.Copy).then_inc(xT_ok, 1)
                if has(-3):
                    sc.wait_ge(w1_ok, s - 2)
                    wait(sc, quant_ok, (s - 3) * 5)
                    activation(xs[:], w1[:].rearrange("p j d -> p (j d)"), ACT.Copy,
                               scale=isc_inv[:, 0:1]).then_inc(xs_ok, 1)
                if has(-2):
                    silu_gate(s - 2, 0)
                if has(2):
                    silu_projection(s + 2, 0)
                if has(2):
                    silu_projection(s + 2, 1)
                if has(2):
                    sc.wait_ge(qkv_ok, (s + 2) * 5 + 2)
                    wait(sc, ssp_ok, s + 2)
                    activation(sqT[:].rearrange("p n t -> p (n t)"), qkvT[:, 0:2, :].rearrange("p n t -> p (n t)"),
                               ACT.Square).then_inc(sqT_ok, 1)
                if has(-2):
                    silu_gate(s - 2, 1)
                if has(2):
                    silu_projection(s + 2, 2)
                if has(2):
                    sc.wait_ge(proj_ok, (s + 2) * 4 + 4)
                    activation(betaT[:], ps_x[0:H, :], ACT.Tanh, scale=0.5).then_inc(qkv_ok, 1)
                if has(-2):
                    silu_gate(s - 2, 2)
                if has(-3):
                    sc.wait_ge(xqtr_ok, s - 2)
                    wait(sc, lin_ok, s - 3)
                    activation(xqT[:], ps_q, ACT.Copy).then_inc(xqT_ok, 1)
                if has(-4):
                    sc.wait_ge(norm_ok, (s + 3) * NORM_OPS)
                    wait(sc, y_stored, (s - 4) * 16 * R)
                    tiles(ACT.Identity, yout, r1, scale_of=rs_r, bias_of=nmean_rs[:, J:2 * J]).then_inc(yout_ok, 1)
                if has(2):
                    sc.wait_ge(qkv_ok, (s + 2) * 5 + 4)
                    activation(betaT[:], betaT[:], ACT.Copy, scale=0.5, bias=0.5).then_inc(qkv_ok, 1)
                if has(2):
                    sc.wait_ge(ssp_ok, s + 3)
                    activation(ssT[P // 2:P, :], ps_x[P // 2:P, :], ACT.Copy).then_inc(ssT_ok, 1)
                if has(-2):
                    silu_gate(s - 2, 3)
                if has(3):
                    wait(sc, norm_ok, (s + 2) * NORM_OPS + NORM_OPS)
                    sc.wait_ge(x_in[1 - par], (pair_of + 1 + par) * (16 * R) + 16 * R)
                    tiles(ACT.Square, xx, xa[1 - par], accum=sumsq[:, COL_X:COL_X + J], scale=RMS).then_inc(ssx_ok, 1)
                if has(-1):
                    sc.wait_ge(norm_ok, (s + 3) * NORM_OPS)
                    sc.wait_ge(h_ok, s)
                    tiles(ACT.Square, hh, h, accum=sumsq[:, COL_H:COL_H + J], scale=RMS).then_inc(ssh_ok, 1)
                if has(-3):
                    sc.wait_ge(r_ok, s - 2)
                    tiles(ACT.Copy, rr[:, 0], r1, accum=nmean[:, J:2 * J], scale=-RMS / D).then_inc(rmean_ok, 1)
                if has(-3):
                    sc.wait_ge(rmean_ok, s - 2)
                    tiles(ACT.Square, rr[:, 1], r1, accum=sumsq[:, COL_R:COL_R + J],
                          bias_of=nmean[:, J:2 * J], scale=RMS).then_inc(ssr_ok, 1)
                if has(1):
                    n = s + 1
                    sc.wait_ge(solve_ok, (n + 1) * SOLVE_OPS)
                    activation(ws_prod[1 - par][:, :, :, :, DK], wu_rows[1 - par][:, :, :, DK:2 * DK],
                               ACT.Copy).then_inc(u_ok, 1)
                if has(-2):
                    sc.wait_ge(z_ok, s - 1)
                    tiles(ACT.Copy, zz[:, 0], z, accum=nmean[:, 0:J], scale=-RMS / D).then_inc(zmean_ok, 1)
                if has(-2):
                    sc.wait_ge(zmean_ok, s - 1)
                    tiles(ACT.Square, zz[:, 1], z, accum=sumsq[:, COL_Z:COL_Z + J],
                          bias_of=nmean[:, 0:J], scale=RMS).then_inc(ssz_ok, 1)

            every_iteration(sc, body)

        @block.gpsimd
        def _(pool):
            tt = nc.gpsimd.tensor_tensor
            for m in (ident, identh, head_sum):
                nc.gpsimd.memset(m[:], 0.0).then_inc(const_ok, 1)
            pool.wait_ge(const_ok, 3)
            for m in (ident, identh):
                nc.gpsimd.affine_select(out=m[:], in_=m[:], compare_op=ALU.not_equal, fill=1.0, base=0,
                                        pattern=[[-1, P]], channel_multiplier=1).then_inc(const_ok, 1)
            nc.gpsimd.memset(head_sum[:, 0:H], 1.0).then_inc(const_ok, 1)
            pool.wait_ge(const_ok, 6)
            nc.gpsimd.affine_select(out=head_sum[:, 0:H], in_=head_sum[:, 0:H], compare_op=ALU.is_ge, fill=0.0, base=0,
                                    pattern=[[-DK, H]], channel_multiplier=1).then_inc(const_ok, 1)
            pool.wait_ge(const_ok, 7)
            nc.gpsimd.affine_select(out=head_sum[:, 0:H], in_=head_sum[:, 0:H], compare_op=ALU.is_ge, fill=0.0,
                                    base=DK - 1, pattern=[[DK, H]], channel_multiplier=-1).then_inc(const_ok, 1)

            def prepare(n, par, s):
                wuv, kbv, qnv = wu_rows[par], kb_rows[par], qn_rows[par]
                pool.wait_ge(raw_in, (n + 1) * LANE_DMAS)
                pool.wait_ge(norm_ok, (s + 3) * NORM_OPS)
                tt(rbeta[:], rs_qk[:, 1], beta[:], ALU.mult).then_inc(rows_ok, 1)
                wait(pool, scan_ok, done(s) * SEG_OPS)
                wait(pool, u_ok, done(s))
                wait(pool, qs_ok, done(s) * 2)

                def scaled(dst, which, r):
                    for sl in range(SL):
                        last = tt(dst[:, :, sl, 0:DK], raw[:, which, sl].rearrange("p d t -> p t d"),
                                  r[:, sl, :].unsqueeze(2).broadcast_to([P, T, DK]), ALU.mult)
                    last.then_inc(rows_ok, 1)

                scaled(wuv, 1, rs_qk[:, 1])
                scaled(qnv, 0, rs_qk[:, 0])
                pool.wait_ge(rows_ok, n * 4 + 1)
                scaled(kbv, 1, rbeta)
                pool.wait_ge(rows_ok, n * 4 + 4)
                wait(pool, pair_ok, n)
                wc = wuv[:].rearrange("p (c i) s e -> p c i s e", i=C)
                kc = kbv[:].rearrange("p (c i) s e -> p c i s e", i=C)
                for delta in range(1, C):
                    rows = slice(PAIR_ROW[delta], PAIR_ROW[delta] + (C - delta) * SL)
                    tt(pair_prod[:, :, rows, :].rearrange("p c (i s) e -> p c i s e", s=SL),
                       wc[:, :, delta:C, :, 0:DK], kc[:, :, 0:C - delta, :, :], ALU.mult).then_inc(pprod_ok, 1)

            def solve(n, par):
                wc = wu_rows[par][:].rearrange("p (c i) s e -> p c i s e", i=C)
                pool.wait_ge(pair_ok, n + 1)
                pool.wait_ge(v_ok, n + 1)
                k = 0
                for j in range(C - 1):
                    for i in range(j + 1, C):
                        row = PAIR_ROW[i - j] + j * SL
                        coef = pair[:, :, row:row + SL].unsqueeze(3).broadcast_to([P, NCH, SL, 2 * DK])
                        wait(pool, solve_ok, n * SOLVE_OPS + k)
                        tt(solve_tmp[:], coef, wc[:, :, j], ALU.mult).then_inc(solve_ok, 1)
                        pool.wait_ge(solve_ok, n * SOLVE_OPS + k + 1)
                        tt(wc[:, :, i], wc[:, :, i], solve_tmp[:], ALU.subtract).then_inc(solve_ok, 1)
                        k += 2

            def read_out(n, par, half):
                t0 = half * HALF
                pool.wait_ge(scan_ok, n * SEG_OPS + (half + 1) * (SEG_OPS // 2))
                wait(pool, osum_ok, n * 2 + half - 1)
                q = qn_rows[par][:, t0:t0 + HALF].unsqueeze(3).broadcast_to([P, HALF, SL, DK, DK])
                tt(qs_prod[half][:].rearrange("p k (t s v) -> p t s v k", s=SL, v=DK),
                   states[:, t0:t0 + HALF].rearrange("p t (s v k) -> p t s v k", s=SL, v=DK),
                   q, ALU.mult).then_inc(qs_ok, 1)

            def body(s, par, pair_of, has):
                if has(-1):
                    read_out(s - 1, 1 - par, 1)
                if has(1):
                    prepare(s + 1, 1 - par, s)
                if has(-3):
                    n = s - 3
                    pool.wait_ge(w1_ok, n + 1)
                    wait(pool, r_ok, n)
                    tt(w1b[:], w1[:], bias_b[:].unsqueeze(1).broadcast_to([P, J, D]), ALU.add).then_inc(w1b_ok, 1)
                if has(1):
                    solve(s + 1, 1 - par)
                if has(0):
                    read_out(s, par, 0)
                if has(-1):
                    n = s - 1
                    pool.wait_ge(xr_in, (n + 1) * 16 * R)
                    pool.wait_ge(h_ok, n + 1)
                    wait(pool, z_ok, n)
                    tt(xh[:], xr[:], h[:], ALU.add).then_inc(xh_ok, 1)

            pool.wait_ge(w_in, WEIGHTS)
            every_iteration(pool, body)

        @block.vector
        def _(dve):
            V = nc.vector
            V.memset(states[:, T - 1, :], 0.0).then_inc(init_ok, 1)
            V.memset(sumsq[:], 1.0).then_inc(init_ok, 1)
            V.memset(nmean[:], 0.0).then_inc(init_ok, 1)
            V.memset(eps[:, 0:COL_Z], RMS_EPS).then_inc(init_ok, 1)
            V.memset(eps[:, COL_Z:COLS], LN_EPS).then_inc(init_ok, 1)
            dve.wait_ge(w_in, WEIGHTS)
            for w, l in ((wq, ln1c), (wk, ln1c), (wv, ln1c), (wb, ln1c), (wg, ln2c), (wu, ln2c)):
                V.tensor_scalar(w[:], w[:], l[:, 0:1], None, ALU.mult).then_inc(w_scaled, 1)
            V.reciprocal(isc_inv[:], isc[:]).then_inc(w_scaled, 1)
            dve.wait_ge(w8_tr, 1)
            V.tensor_scalar(w8t[:], ps_z[:, 0:P], wsc[:, 0:1], isc[:, 0:1], ALU.mult, ALU.mult).then_inc(w_scaled, 1)
            dve.wait_ge(w_scaled, 8)
            V.tensor_copy(w8part[0][:], w8t[:]).then_inc(w_scaled, 1)
            dve.wait_ge(w_scaled, 9)
            V.tensor_tensor(w8t[:], w8t[:], w8part[0][:], ALU.subtract).then_inc(w_scaled, 1)
            dve.wait_ge(w_scaled, 10)
            V.tensor_copy(w8part[1][:], w8t[:]).then_inc(w_scaled, 1)
            dve.wait_ge(w_scaled, 11)
            V.tensor_tensor(w8part[2][:], w8t[:], w8part[1][:], ALU.subtract).then_inc(w_scaled, 1)
            dve.wait_ge(init_ok, 5)

            def flat(t):
                return t[:].rearrange("p j d -> p (j d)")

            def body(s, par, pair_of, has):
                def norm(k):
                    if is_first(s):
                        return
                    base = (s + 2) * NORM_OPS
                    if k == 0:
                        wait(dve, raw_in, done(s + 2) * LANE_DMAS)
                        wait(dve, ssx_ok, done(s + 3))
                        wait(dve, ssh_ok, done(s - 1))
                        wait(dve, ssz_ok, done(s - 2))
                        wait(dve, ssr_ok, done(s - 3))
                        V.tensor_tensor(radicand[:], sumsq[:], eps[:], ALU.add).then_inc(norm_ok, 1)
                        return
                    dve.wait_ge(norm_ok, base + k)
                    if k == 1:
                        wait(dve, xn_ok, done(s + 2))
                        wait(dve, rows_ok, done(s + 1) * 4)
                        wait(dve, y_ok, done(s - 2))
                        wait(dve, w1_ok, done(s - 3))
                        wait(dve, yout_ok, done(s - 4))
                        V.tensor_scalar(rs[:].bitcast(I32), radicand[:].bitcast(I32), -0.5, RSQRT_SEED, ALU.mult,
                                        ALU.add).then_inc(norm_ok, 1)
                    elif k == NORM_OPS - 1:
                        V.scalar_tensor_tensor(out=nmean_rs[:], in0=nmean[:], scalar=float(D) ** 0.5,
                                               in1=rs[:, COL_Z:COLS], op0=ALU.mult, op1=ALU.mult).then_inc(norm_ok, 1)
                    elif k % 3 == 2:
                        V.tensor_tensor(newton[:], rs[:], rs[:], ALU.mult).then_inc(norm_ok, 1)
                    elif k % 3 == 0:
                        V.scalar_tensor_tensor(out=newton[:], in0=newton[:], scalar=-0.5, in1=radicand[:],
                                               op0=ALU.mult, op1=ALU.mult).then_inc(norm_ok, 1)
                    else:
                        V.scalar_tensor_tensor(out=rs[:], in0=newton[:], scalar=1.5, in1=rs[:], op0=ALU.add,
                                               op1=ALU.mult).then_inc(norm_ok, 1)

                def scan(c, k):
                    if not has(0):
                        return
                    base = s * SEG_OPS + c * SCAN_OPS
                    t0 = c * C
                    wait(dve, scan_ok, base + k)
                    if k == 0:
                        if c == 0:
                            dve.wait_ge(u_ok, s + 1)
                        state = states[:, (t0 - 1) % T, :].rearrange("p (s v k) -> p s v k", s=SL, v=DK)
                        V.tensor_tensor(
                            ws_prod[par][:, t0:t0 + C, :, :, 0:DK],
                            wu_rows[par][:, t0:t0 + C, :, 0:DK].unsqueeze(3).broadcast_to([P, C, SL, DK, DK]),
                            state.unsqueeze(1).broadcast_to([P, C, SL, DK, DK]), ALU.mult).then_inc(scan_ok, 1)
                    elif k == 1:
                        V.tensor_reduce(nu[:], ws_prod[par][:, t0:t0 + C], AX_X, ALU.add).then_inc(scan_ok, 1)
                    elif k == 2:
                        V.tensor_tensor(outer[:].rearrange("p c (s v k) -> p c s v k", s=SL, v=DK),
                                        nu[:].unsqueeze(4).broadcast_to([P, C, SL, DK, DK]),
                                        kb_rows[par][:, t0:t0 + C].unsqueeze(3).broadcast_to([P, C, SL, DK, DK]),
                                        ALU.mult).then_inc(scan_ok, 1)
                    else:
                        i = k - 3
                        if i == 0 and c % (NCH // 2) == 0:
                            wait(dve, qs_ok, (s - 1) * 2 + c // (NCH // 2) + 1)
                        V.tensor_tensor(states[:, t0 + i, :], states[:, (t0 + i - 1) % T, :], outer[:, i, :],
                                        ALU.subtract).then_inc(scan_ok, 1)

                def quantise(k):
                    if not has(-3):
                        return
                    n = s - 3
                    if k == 0:
                        dve.wait_ge(xs_ok, n + 1)
                        V.tensor_scalar(xs[:], xs[:], FP8_MAX, -FP8_MAX, ALU.min, ALU.max).then_inc(quant_ok, 1)
                        return
                    dve.wait_ge(quant_ok, n * 5 + k)
                    if k == 1:
                        V.tensor_scalar(magic[:].bitcast(I32), xs[:].bitcast(I32), EXPONENT_BITS, None,
                                        ALU.bitwise_and).then_inc(quant_ok, 1)
                    elif k == 2:
                        V.tensor_scalar(magic[:], magic[:], FP8_MIN_NORMAL, ROUND_TO_4_BITS, ALU.max,
                                        ALU.mult).then_inc(quant_ok, 1)
                    elif k == 3:
                        V.tensor_tensor(xs[:], xs[:], magic[:], ALU.add).then_inc(quant_ok, 1)
                    else:
                        wait(dve, xqtr_ok, n)
                        V.tensor_tensor(flat(xq), xs[:], magic[:], ALU.subtract).then_inc(quant_ok, 1)

                def gated(c):
                    if not has(-2):
                        return
                    n = s - 2
                    dve.wait_ge(silu_ok, n * FC + c + 1)
                    if c == 0:
                        wait(dve, wd_ok, n)
                    V.tensor_tensor(act[:, c, :], gate[c % 2][:], ps_g[(2 * c + 1) % 3][:],
                                    ALU.mult).then_inc(act_ok, 1)

                def pair_sums():
                    if not has(1):
                        return
                    n = s + 1
                    dve.wait_ge(pprod_ok, (n + 1) * (C - 1))
                    wait(dve, solve_ok, n * SOLVE_OPS)
                    V.tensor_reduce(pair[:], pair_prod[:], AX_X, ALU.add).then_inc(pair_ok, 1)

                def residual_h():
                    if not has(-1):
                        return
                    n = s - 1
                    dve.wait_ge(wo_ok, n + 1)
                    dve.wait_ge(xr_in, (n + 1) * 16 * R)
                    wait(dve, y_ok, done(s - 1))
                    wait(dve, xh_ok, n)
                    V.tensor_tensor(flat(h), ps_h[:], flat(xr), ALU.add).then_inc(h_ok, 1)

                def residual_z():
                    if not has(-2):
                        return
                    n = s - 2
                    dve.wait_ge(wd_ok, n + 1)
                    dve.wait_ge(xh_ok, n + 1)
                    wait(dve, w1_ok, done(s - 2))
                    V.tensor_tensor(flat(z), ps_z[:], flat(xh), ALU.add).then_inc(z_ok, 1)

                def residual_r():
                    if not has(-3):
                        return
                    n = s - 3
                    dve.wait_ge(lin_ok, n + 1)
                    dve.wait_ge(w1b_ok, n + 1)
                    wait(dve, yout_ok, done(s - 3))
                    V.tensor_tensor(flat(r1), ps_h[:], flat(w1b), ALU.add).then_inc(r_ok, 1)

                for slot in range(SEG_OPS):
                    scan(slot // SCAN_OPS, slot % SCAN_OPS)
                    if slot in NORM_SLOTS:
                        norm(NORM_SLOTS.index(slot))
                    if slot in QUANT_SLOTS:
                        quantise(QUANT_SLOTS.index(slot))
                    if slot in GATED_SLOTS:
                        gated(GATED_SLOTS.index(slot))
                    if slot == PAIR_SLOT:
                        pair_sums()
                    if slot == H_SLOT:
                        residual_h()
                    if slot == R_SLOT:
                        residual_r()
                    if slot == Z_SLOT:
                        residual_z()

            every_iteration(dve, body)


_INS = ["L0_attn_hidden_states", "L0_attn_Wq", "L0_attn_Wk", "L0_attn_Wv", "L0_attn_Wb", "L0_attn_Wo", "L0_attn_ln1",
        "L0_attn_ln2", "L0_attn_Wg", "L0_attn_Wu", "L0_attn_Wd", "L0_ffn_weight_fp8", "L0_ffn_bias",
        "L0_ffn_input_scale", "L0_ffn_weight_scale"]


def kernel(**inputs):
    import numpy as _np
    import concourse.bacc as _bacc
    from concourse import mybir as _mybir
    from concourse.bass_utils import run_bass_kernel_spmd as _run

    nc = _bacc.Bacc("TRN2", target_bir_lowering=False, num_devices=1)
    arrays, args = {}, []
    for name in _INS:
        a = _np.ascontiguousarray(inputs[name])
        arrays[f"in_{name}"] = a
        args.append(nc.dram_tensor(f"in_{name}", a.shape, _mybir.dt.from_np(a.dtype), kind="ExternalInput").ap())
    shape = inputs[_INS[0]].shape
    result = nc.dram_tensor("out_0", shape, _mybir.dt.float32, kind="ExternalOutput").ap()
    build(nc, *args, result)
    r = _run(nc, [arrays], core_ids=[0])
    return r.results[0]["out_0"]
```

```python
from contextlib import ExitStack

import concourse.bass as bass
from concourse import mybir

P = 128
F32 = mybir.dt.float32
BF16 = mybir.dt.bfloat16
I32 = mybir.dt.int32
ALU = mybir.AluOpType
ACT = mybir.ActivationFunctionType
AX_X = mybir.AxisListType.X

RMS_EPS = 1e-6
LN_EPS = 1e-5
FP8_MAX = 448.0
FP8_MIN_NORMAL = 2.0 ** -6
EXPONENT_BITS = 0x7F800000
ROUND_TO_4_BITS = 1.5 * 2.0 ** 20
RSQRT_SEED = float(0x5F3759DF)
NEWTON_STEPS = 3
NORM_OPS = 3 + 3 * NEWTON_STEPS
NORM_SLOTS = (2, 3, 4, 5, 7, 9, 10, 12, 13, 14, 15, 16)
QUANT_SLOTS = (26, 27, 30, 33, 38)
GATED_SLOTS = (43, 45)
PAIR_SLOT = 32


def build(nc, x, Wq, Wk, Wv, Wb, Wo, ln1, ln2, Wg, Wu, Wd, W8, bias, iscale, wscale, out):
    NB, S, D = x.shape
    H = Wb.shape[1]
    DK = D // H
    F = Wg.shape[1]
    FC = F // P
    PC = 2
    VC = FC - PC
    T = 32
    NSEG = S // T
    C = 4
    NCH = T // C
    SL = NB * H // P
    LB = P // H
    ST = SL * DK * DK
    TOK = NB * T
    J = TOK // P
    R = P // T
    HALF = T // 2
    SCAN_OPS = 3 + C
    SEG_OPS = NCH * SCAN_OPS
    PAIR_ROW = [0] * C
    for j in range(1, C):
        PAIR_ROW[j] = PAIR_ROW[j - 1] + (C - j) * SL
    PAIRS = PAIR_ROW[C - 1]
    SOLVE_OPS = 2 * (C - 1)
    QK = 2 * SL * T
    COL_X, COL_H, COL_Z, COL_R, COLS = (QK + i * J for i in range(5))
    LANE_DMAS = 16 * 3 * SL
    OUT_DMAS = 16 * 6
    assert D == P and F % P == 0 and SL * P == NB * H and TOK == 512 and FC == 4 and NCH == 8

    ctx = ExitStack()
    with ctx:
        def sb(name, shape, dt=F32):
            return ctx.enter_context(nc.sbuf_tensor(name, shape, dt))

        def psum(name):
            return ctx.enter_context(nc.psum_tensor(name, [P, 512], F32))

        def sem(name):
            return ctx.enter_context(nc.semaphore(name))

        wq, wk, wv, wo = (sb(n, [P, D]) for n in ("wq", "wk", "wv", "wo"))
        wb = sb("wb", [P, H])
        wg, wu = sb("wg", [P, F]), sb("wu", [P, F])
        wd = sb("wd", [P, FC, D])
        w8 = sb("w8", [P, D])
        w8t = sb("w8t", [P, D])
        w8part = [sb(f"w8part{i}", [P, D], BF16) for i in range(3)]
        ln1c, ln2c = sb("ln1c", [P, 1]), sb("ln2c", [P, 1])
        isc, wsc, isc_inv = sb("isc", [P, 1]), sb("wsc", [P, 1]), sb("isc_inv", [P, 1])
        bias_b = sb("bias_b", [P, D])
        ident, identh = sb("ident", [P, P]), sb("identh", [P, P], BF16)
        head_sum = sb("head_sum", [P, 2 * H])

        sumsq, eps, radicand, rs, newton = (sb(n, [P, COLS]) for n in ("sumsq", "eps", "radicand", "rs", "newton"))
        nmean, nmean_rs = sb("nmean", [P, 2 * J]), sb("nmean_rs", [P, 2 * J])
        rs_qk = rs[:, 0:QK].rearrange("p (n s t) -> p n s t", n=2, s=SL)
        rs_x, rs_h, rs_z, rs_r = (rs[:, c:c + J] for c in (COL_X, COL_H, COL_Z, COL_R))
        xa = [sb(f"xa{p}", [P, J, D]) for p in range(2)]
        xx = sb("xx", [P, J, D], BF16)
        xn = sb("xn", [P, J, D])
        xT = sb("xT", [P, TOK])
        qkvT = sb("qkvT", [P, 3, TOK])
        betaT = sb("betaT", [H, TOK])
        sqT = sb("sqT", [P, 2, TOK])
        ssT = sb("ssT", [P, TOK])
        raw = sb("raw", [P, 3, SL, DK, T])
        beta = sb("beta", [P, SL, T])
        rbeta = sb("rbeta", [P, SL, T])
        wu_rows = [sb(f"wu_rows{p}", [P, T, SL, 2 * DK]) for p in range(2)]
        kb_rows = [sb(f"kb_rows{p}", [P, T, SL, DK]) for p in range(2)]
        qn_rows = [sb(f"qn_rows{p}", [P, T, SL, DK]) for p in range(2)]
        pair_prod = sb("pair_prod", [P, NCH, PAIRS, DK])
        pair = sb("pair", [P, NCH, PAIRS])
        solve_tmp = sb("solve_tmp", [P, NCH, C - 1, SL, 2 * DK])
        states = sb("states", [P, T, ST])
        ws_prod = [sb(f"ws_prod{p}", [P, T, SL, DK, DK + 1]) for p in range(2)]
        nu = sb("nu", [P, C, SL, DK])
        outer = sb("outer", [P, C, ST])
        qs_prod = [sb(f"qs_prod{i}", [P, DK, HALF * SL * DK]) for i in range(2)]
        o_lane = sb("o_lane", [P, SL, DK, T])
        oT = sb("oT", [P, TOK])
        xr = [sb(f"xr{p}", [P, J, D]) for p in range(2)]
        h = sb("h", [P, J, D])
        hh = sb("hh", [P, J, D], BF16)
        y = sb("y", [P, J, D])
        yT = sb("yT", [P, TOK])
        gate = [sb(f"gate{p}", [P, TOK]) for p in range(2)]
        pool_gate = [sb(f"pool_gate{c}", [P, TOK]) for c in range(PC)]
        pool_up = [sb(f"pool_up{c}", [P, TOK]) for c in range(PC)]
        act = sb("act", [P, FC, TOK])
        zz = sb("zz", [P, 2, J, D], BF16)
        w1 = sb("w1", [P, J, D])
        xs = sb("xs", [P, TOK])
        magic = sb("magic", [P, TOK])
        xq = sb("xq", [P, J, D], BF16)
        xqT = sb("xqT", [P, TOK], BF16)
        w1b = sb("w1b", [P, J, D])
        rr = sb("rr", [P, 2, J, D], BF16)
        yout = sb("yout", [P, J, D])

        ps_x = psum("ps_x")
        ps_p = psum("ps_p")
        ps_oq = psum("ps_oq")
        ps_g = [psum(f"ps_g{i}") for i in range(3)]
        ps_h = psum("ps_h")
        ps_z = psum("ps_z")
        ps_q = ps_oq[:, 0:TOK // 2].bitcast(BF16)
        ps_o = ps_oq[:, TOK // 2:TOK]

        tok_h, tok_z = (ps[:].rearrange("p (j d) -> p j d", j=J) for ps in (ps_h, ps_z))

        d_qkv = nc.dram_tensor("d_qkv", (3, NB, H, DK, T), F32, kind="Internal").ap()
        d_stat = nc.dram_tensor("d_stat", (3, NB, H, T), F32, kind="Internal").ap()
        d_o = nc.dram_tensor("d_o", (NB, H, DK, T), F32, kind="Internal").ap()

        qkv_w_in, w_in, w8_tr = sem("qkv_w_in"), sem("w_in"), sem("w8_tr")
        qkv_w_scaled, w_scaled = sem("qkv_w_scaled"), sem("w_scaled")
        const_ok, init_ok = sem("const_ok"), sem("init_ok")
        norm_ok = sem("norm_ok")
        x_in = [sem(f"x_in{p}") for p in range(2)]
        ssx_ok, xn_ok, xtr_ok, xT_ok = (sem(n) for n in ("ssx_ok", "xn_ok", "xtr_ok", "xT_ok"))
        proj_ok = sem("proj_ok")
        qkv_ok = sem("qkv_ok")
        sqT_ok, ssp_ok, ssT_ok = sem("sqT_ok"), sem("ssp_ok"), sem("ssT_ok")
        qkv_out, raw_in = sem("qkv_out"), sem("raw_in")
        v_ok = sem("v_ok")
        rows_ok = sem("rows_ok")
        pprod_ok, pair_ok = sem("pprod_ok"), sem("pair_ok")
        solve_ok, u_ok = sem("solve_ok"), sem("u_ok")
        scan_ok = sem("scan_ok")
        qs_ok, osum_ok, o_ok = sem("qs_ok"), sem("osum_ok"), sem("o_ok")
        o_out, oT_in = sem("o_out"), sem("oT_in")
        xr_in = [sem(f"xr_in{p}") for p in range(2)]
        wo_ok, h_ok, ssh_ok, zx_ok = (sem(n) for n in ("wo_ok", "h_ok", "ssh_ok", "zx_ok"))
        y_ok, ytr_ok, yT_ok = (sem(n) for n in ("y_ok", "ytr_ok", "yT_ok"))
        gu_ok, silu_ok, act_ok = sem("gu_ok"), sem("silu_ok"), sem("act_ok")
        up_ok, pool_act_ok = sem("up_ok"), sem("pool_act_ok")
        wd_ok, zmean_ok, ssz_ok = (sem(n) for n in ("wd_ok", "zmean_ok", "ssz_ok"))
        w1_ok, xs_ok = sem("w1_ok"), sem("xs_ok")
        quant_ok = sem("quant_ok")
        xqtr_ok, xqT_ok, lin_ok, w1b_ok = (sem(n) for n in ("xqtr_ok", "xqT_ok", "lin_ok", "w1b_ok"))
        rmean_ok, ssr_ok = sem("rmean_ok"), sem("ssr_ok")
        yout_ok, y_stored = sem("yout_ok"), sem("y_stored")

        def wait(eng, s, value):
            if not isinstance(value, int) or value > 0:
                eng.wait_ge(s, value)

        def done(v):
            return max(0, min(v, NSEG)) if isinstance(v, int) else v

        FIRST, LAST = -4, NSEG + 3
        LOOP_FROM, LOOP_PAIRS = 5, (NSEG - 9) // 2

        def is_first(s):
            return isinstance(s, int) and s == FIRST

        def every_iteration(eng, body, before={}):
            def peeled(s):
                if s in before:
                    before[s]()
                body(s, s % 2, s // 2, lambda d: 0 <= s + d < NSEG)
            for s in range(FIRST, LOOP_FROM):
                peeled(s)
            with eng.Fori(0, LOOP_PAIRS) as m:
                body(m * 2 + LOOP_FROM, 1, m + LOOP_FROM // 2, lambda d: True)
                body(m * 2 + LOOP_FROM + 1, 0, m + LOOP_FROM // 2 + 1, lambda d: True)
            for s in range(LOOP_FROM + 2 * LOOP_PAIRS, LAST + 1):
                peeled(s)

        block = ctx.enter_context(nc.Block())
        qkv_loads = [(ln1c[:], ln1.rearrange("(p a) -> p a", a=1)), (wq[:], Wq), (wk[:], Wk), (wv[:], Wv), (wb[:], Wb)]
        loads = [(wo[:], Wo), (wg[:], Wg), (wu[:], Wu), (wd[:], Wd.rearrange("(c p) n -> p c n", p=P)), (w8[:], W8),
                 (ln2c[:], ln2.rearrange("(p a) -> p a", a=1)), (isc[:], iscale.partition_broadcast(P)),
                 (wsc[:], wscale.partition_broadcast(P)), (bias_b[:], bias.partition_broadcast(P))]
        QKV_WEIGHTS, WEIGHTS = 16 * len(qkv_loads), 16 * len(loads)

        @block.sync
        def _(sp):
            def load_x(dst, t0, signal):
                for r in range(R):
                    src = x.rearrange("(j r) t d -> r t j d", r=R)[r]
                    sp.dma_start(dst[r * T:(r + 1) * T, :, :], src[bass.ds(t0, T), :, :]).then_inc(signal, 16)

            def body(s, par, pair_of, has):
                def reg(value):
                    if not isinstance(value, int):
                        sp.compute_val(value)
                    return value

                t_in, t_out, t_res = (reg((s + d) * T) if has(d) else 0 for d in (4, -4, -1))
                a_xn, a_o, a_oout, a_wo, a_qkv, a_st, a_raw, a_out, a_rows, a_v, a_x, a_y, a_norm = (reg(v) for v in (
                    done(s + 3), done(s) * 2, done(s) * 16, done(s - 1), (s + 3) * 5, s + 3, (s + 2) * LANE_DMAS,
                    (s + 3) * OUT_DMAS, done(s + 2) * 4, done(s + 2), done(s - 2), done(s - 3), (s + 3) * NORM_OPS + 1))
                if has(-1):
                    sp.wait_ge(o_ok, a_o)
                    sp.dma_start(d_o.rearrange("(sl b) h v t -> (b h) sl (v t)", sl=SL),
                                 o_lane[:].rearrange("p sl v t -> p sl (v t)")).then_inc(o_out, 16)
                if has(4):
                    wait(sp, xn_ok, a_xn)
                    load_x(xa[par], t_in, x_in[par])
                if has(-1):
                    wait(sp, wo_ok, a_x)
                    wait(sp, zx_ok, a_x)
                    load_x(xr[1 - par], t_res, xr_in[1 - par])
                if has(-1):
                    sp.wait_ge(o_out, a_oout)
                    wait(sp, wo_ok, a_wo)
                    sp.dma_start(oT[:].rearrange("p (b t) -> p b t", b=NB),
                                 d_o.rearrange("b h v t -> (h v) b t")).then_inc(oT_in, 16)
                if has(2):
                    sp.wait_ge(qkv_ok, a_qkv)
                    wait(sp, raw_in, a_raw)
                    for n in range(3):
                        sp.dma_start(d_qkv[n].rearrange("b h d t -> (h d) b t"),
                                     qkvT[:, n, :].rearrange("p (b t) -> p b t", b=NB)).then_inc(qkv_out, 16)
                    sp.dma_start(d_stat[0].rearrange("b h t -> h b t"),
                                 betaT[:].rearrange("p (b t) -> p b t", b=NB)).then_inc(qkv_out, 16)
                if has(2):
                    sp.wait_ge(ssT_ok, a_st)
                    wait(sp, raw_in, a_raw)
                    for n in range(2):
                        row = P // 2 + n * 2 * H
                        sp.dma_start(d_stat[1 + n].rearrange("b h t -> h b t"),
                                     ssT[row:row + H, :].rearrange("p (b t) -> p b t", b=NB)).then_inc(qkv_out, 16)
                if has(2):
                    sp.wait_ge(qkv_out, a_out)
                    wait(sp, rows_ok, a_rows)
                    wait(sp, v_ok, a_v)
                    wait(sp, norm_ok, a_norm)
                    for sl in range(SL):
                        lanes = slice(sl * LB, (sl + 1) * LB)
                        sp.dma_start(sumsq[:, 0:QK].rearrange("p (n s t) -> p n s t", n=2, s=SL)[:, :, sl, :],
                                     d_stat[1:3, lanes].rearrange("n b h t -> (b h) n t")).then_inc(raw_in, 16)
                        sp.dma_start(beta[:, sl, :],
                                     d_stat[0, lanes].rearrange("b h t -> (b h) t")).then_inc(raw_in, 16)
                        sp.dma_start(raw[:, :, sl, :, :].rearrange("p n d t -> p n (d t)"),
                                     d_qkv[:, lanes].rearrange("n b h d t -> (b h) n (d t)")).then_inc(raw_in, 16)

                if has(-4):
                    sp.wait_ge(yout_ok, a_y)
                    for r in range(R):
                        dst = out.rearrange("(j r) t d -> r t j d", r=R)[r]
                        sp.dma_start(dst[bass.ds(t_out, T), :, :],
                                     yout[r * T:(r + 1) * T, :, :]).then_inc(y_stored, 16)
            def load(pairs, signal):
                for dst, src in pairs:
                    sp.dma_start(dst, src).then_inc(signal, 16)

            every_iteration(sp, body, {FIRST + 1: lambda: load(qkv_loads, qkv_w_in),
                                       FIRST + 2: lambda: load(loads, w_in)})
            sp.wait_ge(y_stored, NSEG * 16 * R)

        @block.tensor
        def _(pe):
            mm = nc.tensor.matmul

            def transposes(dst, src, identity, signal):
                for j in range(J):
                    last = nc.tensor.transpose(dst[:, j * P:(j + 1) * P], src[:, j, :], identity[:])
                last.then_inc(signal, 1)

            def sum_read_out(n, half):
                pe.wait_ge(qs_ok, n * 2 + half + 1)
                wait(pe, o_ok, n * 2 + half)
                for k in range(DK):
                    last = mm(ps_o, ident[:], qs_prod[half][:, k, :], start=(k == 0), stop=(k == DK - 1))
                last.then_inc(osum_ok, 1)

            def gate_up(n, c):
                if c == 0:
                    pe.wait_ge(yT_ok, n + 1)
                    wait(pe, act_ok, n * VC)
                for i, w in ((2 * c, wg), (2 * c + 1, wu)):
                    if i >= 3 and i % 2:
                        pe.wait_ge(silu_ok, n * FC + (i - 3) // 2 + 1)
                    elif i >= 3 and (i - 3) // 2 < PC:
                        pe.wait_ge(up_ok, n * PC + (i - 3) // 2 + 1)
                    elif i >= 3:
                        pe.wait_ge(act_ok, n * VC + (i - 3) // 2 - PC + 1)
                    last = mm(ps_g[i % 3][:], w[:, c * P:(c + 1) * P], yT[:], start=True, stop=True)
                last.then_inc(gu_ok, 1)

            def project(n, i):
                w = (wq, wk, wv, wb)[i]
                if i == 0:
                    pe.wait_ge(xT_ok, n + 1)
                    wait(pe, qkv_ok, n * 5)
                elif i >= 2:
                    pe.wait_ge(qkv_ok, n * 5 + i - 1)
                mm((ps_p, ps_x)[i % 2][0:w.shape[1], :], w[:], xT[:], start=True, stop=True).then_inc(proj_ok, 1)

            def add(dst, src, start):
                return mm(dst[:], ident[:], src[:].rearrange("p j d -> p (j d)"), start=start, stop=False)

            def attention_out(n):
                pe.wait_ge(oT_in, n * 16 + 16)
                for j in range(J):
                    last = mm(ps_h[:, j * P:(j + 1) * P], oT[:, j * P:(j + 1) * P], wo[:], start=False,
                              stop=(j == J - 1))
                last.then_inc(wo_ok, 1)

            def sum_heads(n):
                pe.wait_ge(sqT_ok, n + 1)
                pe.wait_ge(qkv_ok, n * 5 + 2)
                for i in range(2):
                    row = P // 2 + i * 2 * H
                    last = mm(ps_x[row:row + 2 * H, :], head_sum[:], sqT[:, i, :], start=True, stop=True)
                last.then_inc(ssp_ok, 1)

            def linear(n):
                pe.wait_ge(xqT_ok, n + 1)
                for j in range(J):
                    for i, w in enumerate(w8part):
                        last = mm(ps_h[:, j * P:(j + 1) * P], xqT[:, j * P:(j + 1) * P], w[:],
                                  start=False, stop=(j == J - 1 and i == 2))
                last.then_inc(lin_ok, 1)

            def down(n):
                pe.wait_ge(act_ok, n * VC + VC)
                pe.wait_ge(pool_act_ok, n * PC + PC)
                for j in range(J):
                    for c in range(FC):
                        last = mm(ps_z[:, j * P:(j + 1) * P], act[:, c, j * P:(j + 1) * P], wd[:, c, :],
                                  start=False, stop=(j == J - 1 and c == FC - 1))
                last.then_inc(wd_ok, 1)

            pe.wait_ge(const_ok, 8)
            pe.wait_ge(qkv_w_scaled, 4)

            def transpose_w8():
                pe.wait_ge(w_in, WEIGHTS)
                nc.tensor.transpose(ps_z[:, 0:P], w8[:], ident[:]).then_inc(w8_tr, 1)


            def body(s, par, pair_of, has):
                if has(2):
                    pe.wait_ge(xn_ok, s + 3)
                    wait(pe, qkv_ok, (s + 2) * 5)
                    wait(pe, ssT_ok, s + 2)
                    transposes(ps_x, xn, ident, xtr_ok)
                if has(-1):
                    sum_read_out(s - 1, 0)
                if has(2):
                    project(s + 2, 0)
                if has(2):
                    project(s + 2, 1)
                if has(2):
                    project(s + 2, 2)
                if has(2):
                    project(s + 2, 3)
                if has(-1):
                    sum_read_out(s - 1, 1)
                if has(2):
                    sum_heads(s + 2)
                if has(-2):
                    pe.wait_ge(y_ok, s - 1)
                    wait(pe, act_ok, (s - 2) * VC)
                    transposes(ps_g[2], y, ident, ytr_ok)
                if has(-2):
                    n = s - 2
                    pe.wait_ge(h_ok, n + 1)
                    pe.wait_ge(xr_in[par], pair_of * (16 * R))
                    wait(pe, w1_ok, n)
                    add(ps_z, xr[par], True)
                    add(ps_z, h, False).then_inc(zx_ok, 1)
                if has(-2):
                    gate_up(s - 2, 0)
                if has(-2):
                    gate_up(s - 2, 1)
                if has(-1):
                    pe.wait_ge(xr_in[1 - par], (pair_of + par) * (16 * R))
                    wait(pe, yout_ok, done(s - 3))
                    wait(pe, h_ok, s - 1)
                    add(ps_h, xr[1 - par], True)
                if has(-1):
                    attention_out(s - 1)
                if has(-2):
                    gate_up(s - 2, 2)
                if has(-3):
                    pe.wait_ge(quant_ok, (s - 3) * 5 + 5)
                    wait(pe, xqT_ok, s - 3)
                    transposes(ps_q, xq, identh, xqtr_ok)
                if has(-2):
                    gate_up(s - 2, 3)
                if has(-3):
                    pe.wait_ge(w1b_ok, s - 2)
                    wait(pe, h_ok, done(s))
                    wait(pe, yout_ok, s - 3)
                    add(ps_h, w1b, True)
                if has(-3):
                    linear(s - 3)
                if has(-2):
                    down(s - 2)

            every_iteration(pe, body, {-1: transpose_w8, 1: lambda: pe.wait_ge(w_scaled, 8)})

        @block.scalar
        def _(sc):
            activation = nc.scalar.activation
            RMS = float(D) ** -0.5

            def tiles(func, dst, src, accum=None, bias_of=None, scale_of=None, scale=1.0):
                for j in range(J):
                    more = {} if accum is None else {"accum_out": accum[:, j:j + 1]}
                    if bias_of is not None:
                        more["bias"] = bias_of[:, j:j + 1]
                    last = activation(dst[:, j, :], src[:, j, :], func,
                                      scale=scale if scale_of is None else scale_of[:, j:j + 1], **more)
                return last

            def copy_sums(n, half):
                sc.wait_ge(osum_ok, n * 2 + half + 1)
                if half == 0:
                    wait(sc, o_out, n * 16)
                t0 = half * HALF
                activation(o_lane[:, :, :, t0:t0 + HALF].rearrange("p s v t -> p t (s v)"),
                           ps_o.rearrange("p (t e) -> p t e", t=HALF), ACT.Copy).then_inc(o_ok, 1)

            def silu_gate(n, c):
                sc.wait_ge(gu_ok, n * FC + c + 1)
                if c < PC:
                    wait(sc, pool_act_ok, (n - 1) * PC + c + 1)
                    activation(pool_gate[c][:], ps_g[2 * c % 3][:], ACT.Silu).then_inc(silu_ok, 1)
                    activation(pool_up[c][:], ps_g[(2 * c + 1) % 3][:], ACT.Copy).then_inc(up_ok, 1)
                else:
                    wait(sc, act_ok, n * VC + max(c - 1 - PC, 0))
                    activation(gate[c % 2][:], ps_g[2 * c % 3][:], ACT.Silu).then_inc(silu_ok, 1)

            sc.wait_ge(init_ok, 4)

            def silu_projection(n, i):
                if i == 0:
                    wait(sc, qkv_out, n * OUT_DMAS)
                sc.wait_ge(proj_ok, n * 4 + i + 1)
                activation(qkvT[:, i, :], (ps_p, ps_x)[i % 2][:], ACT.Silu).then_inc(qkv_ok, 1)

            def body(s, par, pair_of, has):
                if has(2):
                    sc.wait_ge(xtr_ok, s + 3)
                    wait(sc, proj_ok, (s + 2) * 4)
                    activation(xT[:], ps_x[:], ACT.Copy).then_inc(xT_ok, 1)
                if has(2):
                    silu_projection(s + 2, 0)
                if has(2):
                    silu_projection(s + 2, 1)
                if has(-1):
                    copy_sums(s - 1, 0)
                if has(2):
                    sc.wait_ge(qkv_ok, (s + 2) * 5 + 2)
                    wait(sc, ssp_ok, s + 2)
                    activation(sqT[:].rearrange("p n t -> p (n t)"), qkvT[:, 0:2, :].rearrange("p n t -> p (n t)"),
                               ACT.Square).then_inc(sqT_ok, 1)
                if has(2):
                    silu_projection(s + 2, 2)
                if has(2):
                    sc.wait_ge(proj_ok, (s + 2) * 4 + 4)
                    activation(betaT[:], ps_x[0:H, :], ACT.Tanh, scale=0.5).then_inc(qkv_ok, 1)
                if has(1):
                    n = s + 1
                    sc.wait_ge(raw_in, (n + 1) * LANE_DMAS)
                    wait(sc, scan_ok, done(s) * SEG_OPS)
                    wait(sc, u_ok, done(s))
                    for sl in range(SL):
                        last = activation(wu_rows[1 - par][:, :, sl, DK:2 * DK],
                                          raw[:, 2, sl, :, :].rearrange("p d t -> p t d"), ACT.Copy, scale=-1.0)
                    last.then_inc(v_ok, 1)
                if has(2):
                    sc.wait_ge(qkv_ok, (s + 2) * 5 + 4)
                    activation(betaT[:], betaT[:], ACT.Copy, scale=0.5, bias=0.5).then_inc(qkv_ok, 1)
                if has(-2):
                    sc.wait_ge(norm_ok, (s + 4) * NORM_OPS)
                    wait(sc, ytr_ok, s - 2)
                    tiles(ACT.Copy, y, h, scale_of=rs_h).then_inc(y_ok, 1)
                if has(-3):
                    sc.wait_ge(norm_ok, (s + 4) * NORM_OPS)
                    wait(sc, w1b_ok, s - 3)
                    tiles(ACT.Identity, w1, tok_z, scale_of=rs_z, bias_of=nmean_rs[:, 0:J]).then_inc(w1_ok, 1)
                if has(-1):
                    copy_sums(s - 1, 1)
                if has(-2):
                    sc.wait_ge(ytr_ok, s - 1)
                    wait(sc, gu_ok, (s - 2) * FC)
                    activation(yT[:], ps_g[2][:], ACT.Copy).then_inc(yT_ok, 1)
                if has(-3):
                    sc.wait_ge(w1_ok, s - 2)
                    wait(sc, quant_ok, (s - 3) * 5)
                    activation(xs[:], w1[:].rearrange("p j d -> p (j d)"), ACT.Copy,
                               scale=isc_inv[:, 0:1]).then_inc(xs_ok, 1)
                if has(-4):
                    sc.wait_ge(norm_ok, (s + 4) * NORM_OPS)
                    wait(sc, y_stored, (s - 4) * 16 * R)
                    tiles(ACT.Identity, yout, tok_h, scale_of=rs_r, bias_of=nmean_rs[:, J:2 * J]).then_inc(yout_ok, 1)
                if has(2):
                    sc.wait_ge(ssp_ok, s + 3)
                    activation(ssT[P // 2:P, :], ps_x[P // 2:P, :], ACT.Copy).then_inc(ssT_ok, 1)
                if has(3):
                    sc.wait_ge(norm_ok, (s + 4) * NORM_OPS)
                    wait(sc, xtr_ok, s + 3)
                    tiles(ACT.Copy, xn, xa[1 - par], scale_of=rs_x).then_inc(xn_ok, 1)
                if has(-2):
                    silu_gate(s - 2, 0)
                if has(-2):
                    silu_gate(s - 2, 1)
                if has(-1):
                    sc.wait_ge(wo_ok, s)
                    wait(sc, y_ok, done(s - 1))
                    wait(sc, zx_ok, done(s - 1))
                    wait(sc, ssh_ok, s - 1)
                    activation(h[:], tok_h, ACT.Copy).then_inc(h_ok, 1)
                if has(-1):
                    sc.wait_ge(norm_ok, (s + 4) * NORM_OPS)
                    sc.wait_ge(h_ok, s)
                    tiles(ACT.Square, hh, h, accum=sumsq[:, COL_H:COL_H + J], scale=RMS).then_inc(ssh_ok, 1)
                if has(-2):
                    silu_gate(s - 2, 2)
                if has(-3):
                    sc.wait_ge(xqtr_ok, s - 2)
                    wait(sc, lin_ok, s - 3)
                    activation(xqT[:], ps_q, ACT.Copy).then_inc(xqT_ok, 1)
                if has(4):
                    wait(sc, norm_ok, (s + 3) * NORM_OPS + 1)
                    sc.wait_ge(x_in[par], (pair_of + 3) * (16 * R))
                    tiles(ACT.Square, xx, xa[par], accum=sumsq[:, COL_X:COL_X + J], scale=RMS).then_inc(ssx_ok, 1)
                if has(-2):
                    silu_gate(s - 2, 3)
                if has(-3):
                    sc.wait_ge(norm_ok, (s + 4) * NORM_OPS)
                    sc.wait_ge(lin_ok, s - 2)
                    tiles(ACT.Copy, rr[:, 0], tok_h, accum=nmean[:, J:2 * J], scale=-RMS / D).then_inc(rmean_ok, 1)
                if has(-3):
                    sc.wait_ge(rmean_ok, s - 2)
                    tiles(ACT.Square, rr[:, 1], tok_h, accum=sumsq[:, COL_R:COL_R + J],
                          bias_of=nmean[:, J:2 * J], scale=RMS).then_inc(ssr_ok, 1)
                if has(1):
                    n = s + 1
                    sc.wait_ge(solve_ok, (n + 1) * SOLVE_OPS)
                    activation(ws_prod[1 - par][:, :, :, :, DK], wu_rows[1 - par][:, :, :, DK:2 * DK],
                               ACT.Copy).then_inc(u_ok, 1)
                if has(-2):
                    sc.wait_ge(norm_ok, (s + 4) * NORM_OPS)
                    sc.wait_ge(wd_ok, s - 1)
                    tiles(ACT.Copy, zz[:, 0], tok_z, accum=nmean[:, 0:J], scale=-RMS / D).then_inc(zmean_ok, 1)
                if has(-2):
                    sc.wait_ge(zmean_ok, s - 1)
                    tiles(ACT.Square, zz[:, 1], tok_z, accum=sumsq[:, COL_Z:COL_Z + J],
                          bias_of=nmean[:, 0:J], scale=RMS).then_inc(ssz_ok, 1)

            every_iteration(sc, body, {3: lambda: sc.wait_ge(w_scaled, 8)})

        @block.gpsimd
        def _(pool):
            tt = nc.gpsimd.tensor_tensor
            for m in (ident, identh, head_sum):
                nc.gpsimd.memset(m[:], 0.0).then_inc(const_ok, 1)
            pool.wait_ge(const_ok, 3)
            for m in (ident, identh):
                nc.gpsimd.affine_select(out=m[:], in_=m[:], compare_op=ALU.not_equal, fill=1.0, base=0,
                                        pattern=[[-1, P]], channel_multiplier=1).then_inc(const_ok, 1)
            nc.gpsimd.memset(head_sum[:, 0:H], 1.0).then_inc(const_ok, 1)
            pool.wait_ge(const_ok, 6)
            nc.gpsimd.affine_select(out=head_sum[:, 0:H], in_=head_sum[:, 0:H], compare_op=ALU.is_ge, fill=0.0, base=0,
                                    pattern=[[-DK, H]], channel_multiplier=1).then_inc(const_ok, 1)
            pool.wait_ge(const_ok, 7)
            nc.gpsimd.affine_select(out=head_sum[:, 0:H], in_=head_sum[:, 0:H], compare_op=ALU.is_ge, fill=0.0,
                                    base=DK - 1, pattern=[[DK, H]], channel_multiplier=-1).then_inc(const_ok, 1)

            def scaled(dst, which, r):
                for sl in range(SL):
                    last = tt(dst[:, :, sl, 0:DK], raw[:, which, sl].rearrange("p d t -> p t d"),
                              r[:, sl, :].unsqueeze(2).broadcast_to([P, T, DK]), ALU.mult)
                last.then_inc(rows_ok, 1)

            def prepare(n, par, s):
                wuv, kbv = wu_rows[par], kb_rows[par]
                pool.wait_ge(raw_in, (n + 1) * LANE_DMAS)
                pool.wait_ge(norm_ok, (s + 4) * NORM_OPS)
                tt(rbeta[:], rs_qk[:, 1], beta[:], ALU.mult).then_inc(rows_ok, 1)
                wait(pool, scan_ok, done(s) * SEG_OPS)
                wait(pool, u_ok, done(s))
                scaled(wuv, 1, rs_qk[:, 1])
                pool.wait_ge(rows_ok, n * 4 + 1)
                scaled(kbv, 1, rbeta)
                pool.wait_ge(rows_ok, n * 4 + 3)
                wait(pool, pair_ok, n)
                wc = wuv[:].rearrange("p (c i) s e -> p c i s e", i=C)
                kc = kbv[:].rearrange("p (c i) s e -> p c i s e", i=C)
                for j in range(C - 1):
                    rows = pair_prod[:, :, PAIR_ROW[j]:PAIR_ROW[j + 1], :]
                    tt(rows.rearrange("p c (i s) e -> p c i s e", s=SL), wc[:, :, j + 1:C, :, 0:DK],
                       kc[:, :, j:j + 1].broadcast_to([P, NCH, C - 1 - j, SL, DK]), ALU.mult).then_inc(pprod_ok, 1)

            def solve(n, par):
                wc = wu_rows[par][:].rearrange("p (c i) s e -> p c i s e", i=C)
                pool.wait_ge(pair_ok, n + 1)
                pool.wait_ge(v_ok, n + 1)
                for j in range(C - 1):
                    shape = [P, NCH, C - 1 - j, SL, 2 * DK]
                    coef = pair[:, :, PAIR_ROW[j]:PAIR_ROW[j + 1]].rearrange("p c (i s) -> p c i s", s=SL)
                    tmp = solve_tmp[:, :, 0:C - 1 - j]
                    wait(pool, solve_ok, n * SOLVE_OPS + 2 * j)
                    tt(tmp, coef.unsqueeze(4).broadcast_to(shape), wc[:, :, j:j + 1].broadcast_to(shape),
                       ALU.mult).then_inc(solve_ok, 1)
                    pool.wait_ge(solve_ok, n * SOLVE_OPS + 2 * j + 1)
                    tt(wc[:, :, j + 1:C], wc[:, :, j + 1:C], tmp, ALU.subtract).then_inc(solve_ok, 1)

            def gated(n, c):
                pool.wait_ge(silu_ok, n * FC + c + 1)
                pool.wait_ge(up_ok, n * PC + c + 1)
                wait(pool, wd_ok, n)
                tt(act[:, c, :], pool_gate[c][:], pool_up[c][:], ALU.mult).then_inc(pool_act_ok, 1)

            def read_out(n, par, half):
                t0 = half * HALF
                pool.wait_ge(scan_ok, n * SEG_OPS + (half + 1) * (SEG_OPS // 2))
                pool.wait_ge(rows_ok, n * 4 + 4)
                wait(pool, osum_ok, n * 2 + half - 1)
                q = qn_rows[par][:, t0:t0 + HALF].unsqueeze(3).broadcast_to([P, HALF, SL, DK, DK])
                tt(qs_prod[half][:].rearrange("p k (t s v) -> p t s v k", s=SL, v=DK),
                   states[:, t0:t0 + HALF].rearrange("p t (s v k) -> p t s v k", s=SL, v=DK),
                   q, ALU.mult).then_inc(qs_ok, 1)

            def body(s, par, pair_of, has):
                if has(-1):
                    read_out(s - 1, 1 - par, 1)
                if has(1):
                    prepare(s + 1, 1 - par, s)
                if has(1):
                    wait(pool, qs_ok, done(s) * 2)
                    scaled(qn_rows[1 - par], 0, rs_qk[:, 0])
                if has(-3):
                    n = s - 3
                    pool.wait_ge(w1_ok, n + 1)
                    wait(pool, lin_ok, n)
                    tt(w1b[:], w1[:], bias_b[:].unsqueeze(1).broadcast_to([P, J, D]), ALU.add).then_inc(w1b_ok, 1)
                if has(-2):
                    gated(s - 2, 0)
                if has(-2):
                    gated(s - 2, 1)
                if has(1):
                    solve(s + 1, 1 - par)
                if has(0):
                    read_out(s, par, 0)

            every_iteration(pool, body, {3: lambda: pool.wait_ge(w_in, WEIGHTS)})

        @block.vector
        def _(dve):
            V = nc.vector
            V.memset(states[:, T - 1, :], 0.0).then_inc(init_ok, 1)
            V.memset(sumsq[:], 1.0).then_inc(init_ok, 1)
            V.memset(nmean[:], 0.0).then_inc(init_ok, 1)
            V.memset(eps[:, 0:COL_Z], RMS_EPS).then_inc(init_ok, 1)
            V.memset(eps[:, COL_Z:COLS], LN_EPS).then_inc(init_ok, 1)

            def scale_qkv_weights():
                dve.wait_ge(qkv_w_in, QKV_WEIGHTS)
                for w in (wq, wk, wv, wb):
                    V.tensor_scalar(w[:], w[:], ln1c[:, 0:1], None, ALU.mult).then_inc(qkv_w_scaled, 1)

            def scale_weights():
                dve.wait_ge(w_in, WEIGHTS)
                for w in (wg, wu):
                    V.tensor_scalar(w[:], w[:], ln2c[:, 0:1], None, ALU.mult).then_inc(w_scaled, 1)
                V.reciprocal(isc_inv[:], isc[:]).then_inc(w_scaled, 1)
                dve.wait_ge(w8_tr, 1)
                V.tensor_scalar(w8t[:], ps_z[:, 0:P], wsc[:, 0:1], isc[:, 0:1], ALU.mult,
                                ALU.mult).then_inc(w_scaled, 1)
                dve.wait_ge(w_scaled, 4)
                V.tensor_copy(w8part[0][:], w8t[:]).then_inc(w_scaled, 1)
                dve.wait_ge(w_scaled, 5)
                V.tensor_tensor(w8t[:], w8t[:], w8part[0][:], ALU.subtract).then_inc(w_scaled, 1)
                dve.wait_ge(w_scaled, 6)
                V.tensor_copy(w8part[1][:], w8t[:]).then_inc(w_scaled, 1)
                dve.wait_ge(w_scaled, 7)
                V.tensor_tensor(w8part[2][:], w8t[:], w8part[1][:], ALU.subtract).then_inc(w_scaled, 1)

            dve.wait_ge(init_ok, 5)

            def flat(t):
                return t[:].rearrange("p j d -> p (j d)")

            def body(s, par, pair_of, has):
                def norm(k):
                    if is_first(s):
                        return
                    base = (s + 3) * NORM_OPS
                    if k == 0:
                        wait(dve, raw_in, done(s + 2) * LANE_DMAS)
                        wait(dve, ssx_ok, done(s + 4))
                        wait(dve, ssh_ok, done(s - 1))
                        wait(dve, ssz_ok, done(s - 2))
                        wait(dve, ssr_ok, done(s - 3))
                        V.tensor_tensor(radicand[:], sumsq[:], eps[:], ALU.add).then_inc(norm_ok, 1)
                        return
                    dve.wait_ge(norm_ok, base + k)
                    if k == 1:
                        wait(dve, xn_ok, done(s + 3))
                        wait(dve, rows_ok, done(s + 1) * 4)
                        wait(dve, y_ok, done(s - 2))
                        wait(dve, w1_ok, done(s - 3))
                        wait(dve, yout_ok, done(s - 4))
                        V.tensor_scalar(rs[:].bitcast(I32), radicand[:].bitcast(I32), -0.5, RSQRT_SEED, ALU.mult,
                                        ALU.add).then_inc(norm_ok, 1)
                    elif k == NORM_OPS - 1:
                        V.scalar_tensor_tensor(out=nmean_rs[:], in0=nmean[:], scalar=float(D) ** 0.5,
                                               in1=rs[:, COL_Z:COLS], op0=ALU.mult, op1=ALU.mult).then_inc(norm_ok, 1)
                    elif k % 3 == 2:
                        V.tensor_tensor(newton[:], rs[:], rs[:], ALU.mult).then_inc(norm_ok, 1)
                    elif k % 3 == 0:
                        V.scalar_tensor_tensor(out=newton[:], in0=newton[:], scalar=-0.5, in1=radicand[:],
                                               op0=ALU.mult, op1=ALU.mult).then_inc(norm_ok, 1)
                    else:
                        V.scalar_tensor_tensor(out=rs[:], in0=newton[:], scalar=1.5, in1=rs[:], op0=ALU.add,
                                               op1=ALU.mult).then_inc(norm_ok, 1)

                def scan(c, k):
                    if not has(0):
                        return
                    base = s * SEG_OPS + c * SCAN_OPS
                    t0 = c * C
                    wait(dve, scan_ok, base + k)
                    if k == 0:
                        if c == 0:
                            dve.wait_ge(u_ok, s + 1)
                        state = states[:, (t0 - 1) % T, :].rearrange("p (s v k) -> p s v k", s=SL, v=DK)
                        V.tensor_tensor(
                            ws_prod[par][:, t0:t0 + C, :, :, 0:DK],
                            wu_rows[par][:, t0:t0 + C, :, 0:DK].unsqueeze(3).broadcast_to([P, C, SL, DK, DK]),
                            state.unsqueeze(1).broadcast_to([P, C, SL, DK, DK]), ALU.mult).then_inc(scan_ok, 1)
                    elif k == 1:
                        V.tensor_reduce(nu[:], ws_prod[par][:, t0:t0 + C], AX_X, ALU.add).then_inc(scan_ok, 1)
                    elif k == 2:
                        V.tensor_tensor(outer[:].rearrange("p c (s v k) -> p c s v k", s=SL, v=DK),
                                        nu[:].unsqueeze(4).broadcast_to([P, C, SL, DK, DK]),
                                        kb_rows[par][:, t0:t0 + C].unsqueeze(3).broadcast_to([P, C, SL, DK, DK]),
                                        ALU.mult).then_inc(scan_ok, 1)
                    else:
                        i = k - 3
                        if i == 0 and c % (NCH // 2) == 0:
                            wait(dve, qs_ok, (s - 1) * 2 + c // (NCH // 2) + 1)
                        V.tensor_tensor(states[:, t0 + i, :], states[:, (t0 + i - 1) % T, :], outer[:, i, :],
                                        ALU.subtract).then_inc(scan_ok, 1)

                def quantise(k):
                    if not has(-3):
                        return
                    n = s - 3
                    if k == 0:
                        dve.wait_ge(xs_ok, n + 1)
                        V.tensor_scalar(xs[:], xs[:], FP8_MAX, -FP8_MAX, ALU.min, ALU.max).then_inc(quant_ok, 1)
                        return
                    dve.wait_ge(quant_ok, n * 5 + k)
                    if k == 1:
                        V.tensor_scalar(magic[:].bitcast(I32), xs[:].bitcast(I32), EXPONENT_BITS, None,
                                        ALU.bitwise_and).then_inc(quant_ok, 1)
                    elif k == 2:
                        V.tensor_scalar(magic[:], magic[:], FP8_MIN_NORMAL, ROUND_TO_4_BITS, ALU.max,
                                        ALU.mult).then_inc(quant_ok, 1)
                    elif k == 3:
                        V.tensor_tensor(xs[:], xs[:], magic[:], ALU.add).then_inc(quant_ok, 1)
                    else:
                        wait(dve, xqtr_ok, n)
                        V.tensor_tensor(flat(xq), xs[:], magic[:], ALU.subtract).then_inc(quant_ok, 1)

                def gated(c):
                    if not has(-2):
                        return
                    n = s - 2
                    dve.wait_ge(silu_ok, n * FC + c + 1)
                    if c == PC:
                        wait(dve, wd_ok, n)
                    V.tensor_tensor(act[:, c, :], gate[c % 2][:], ps_g[(2 * c + 1) % 3][:],
                                    ALU.mult).then_inc(act_ok, 1)

                def pair_sums():
                    if not has(1):
                        return
                    n = s + 1
                    dve.wait_ge(pprod_ok, (n + 1) * (C - 1))
                    wait(dve, solve_ok, n * SOLVE_OPS)
                    V.tensor_reduce(pair[:], pair_prod[:], AX_X, ALU.add).then_inc(pair_ok, 1)

                for slot in range(SEG_OPS):
                    scan(slot // SCAN_OPS, slot % SCAN_OPS)
                    if slot in NORM_SLOTS:
                        norm(NORM_SLOTS.index(slot))
                    if slot in QUANT_SLOTS:
                        quantise(QUANT_SLOTS.index(slot))
                    if slot in GATED_SLOTS:
                        gated(PC + GATED_SLOTS.index(slot))
                    if slot == PAIR_SLOT:
                        pair_sums()

            every_iteration(dve, body, {-2: scale_qkv_weights, -1: scale_weights})


_INS = ["L0_attn_hidden_states", "L0_attn_Wq", "L0_attn_Wk", "L0_attn_Wv", "L0_attn_Wb", "L0_attn_Wo", "L0_attn_ln1",
        "L0_attn_ln2", "L0_attn_Wg", "L0_attn_Wu", "L0_attn_Wd", "L0_ffn_weight_fp8", "L0_ffn_bias",
        "L0_ffn_input_scale", "L0_ffn_weight_scale"]


def kernel(**inputs):
    import numpy as _np
    import concourse.bacc as _bacc
    from concourse import mybir as _mybir
    from concourse.bass_utils import run_bass_kernel_spmd as _run

    nc = _bacc.Bacc("TRN2", target_bir_lowering=False, num_devices=1)
    arrays, args = {}, []
    for name in _INS:
        a = _np.ascontiguousarray(inputs[name])
        arrays[f"in_{name}"] = a
        args.append(nc.dram_tensor(f"in_{name}", a.shape, _mybir.dt.from_np(a.dtype), kind="ExternalInput").ap())
    shape = inputs[_INS[0]].shape
    result = nc.dram_tensor("out_0", shape, _mybir.dt.float32, kind="ExternalOutput").ap()
    build(nc, *args, result)
    r = _run(nc, [arrays], core_ids=[0])
    return r.results[0]["out_0"]
```
